# Optimizing a Trainium2 kernel written in Bass

```python
import numpy as np
import jax
import jax.numpy as jnp

def _softmax(x, axis=-1):
    return jax.nn.softmax(x, axis=axis)

def _gelu(x):
    return jax.nn.gelu(x, approximate=True)

def _silu(x):
    return jax.nn.silu(x)

def _sigmoid(x):
    return jax.nn.sigmoid(x)

def _layernorm(x, axis=-1, eps=1e-05):
    m = jnp.mean(x, axis=axis, keepdims=True)
    v = jnp.var(x, axis=axis, keepdims=True)
    return (x - m) / jnp.sqrt(v + eps)

def _scatter_add(tgt, idx, src, axis=0):
    return tgt.at[idx].add(src)

def _segment_sum(src, seg, n):
    return jax.ops.segment_sum(src, seg, n)
kernel_name = 'mk_gnn_preln_d2_gnn_r8_68f4c5'

def setup_inputs(seed: int=0):
    np.random.seed(seed)
    _w = jnp.asarray

    def _rec_inputs():
        import jax
        import jax.numpy as jnp
        _gk = jax.random.key(seed)
        x = -0.0003713 + 1 * jax.random.normal(jax.random.fold_in(_gk, 1), (12500, 256), jnp.float32)
        _s = jax.random.randint(jax.random.fold_in(_gk, 2), (100000,), 0, 12500, jnp.int32)
        _d = jax.random.randint(jax.random.fold_in(_gk, 3), (100000,), 0, 12500, jnp.int32)
        _loop = jnp.arange(12500, dtype=jnp.int32)
        src = jnp.concatenate([_s, _d, _loop])
        dst = jnp.concatenate([_d, _s, _loop])
        _o = jnp.argsort(dst, stable=True)
        src = src[_o]
        dst = dst[_o]
        edge_type_8 = jax.random.randint(jax.random.fold_in(_gk, 12), (212500,), 0, 8, jnp.int32)
        edge_weight = jax.random.uniform(jax.random.fold_in(_gk, 13), (212500,), jnp.float32, 0.0, 0.999999)
        return (x, src, dst, edge_type_8, edge_weight)
    x, src, dst, edge_type_8, edge_weight = _rec_inputs()

    def _L0_gnn_setup():
        import jax, jax.numpy as jnp
        import numpy as np
        N = 6250
        E = 100000
        IN_C = 256
        HID = 64
        HEADS = 4
        NEG_SLOPE = 0.2

        def _gat_conv(x, W, att_src, att_dst, b, src, dst):
            n = x.shape[0]
            h = (x @ W).reshape(n, HEADS, HID)
            a_s = jnp.einsum('nhc,hc->nh', h, att_src)
            a_d = jnp.einsum('nhc,hc->nh', h, att_dst)
            e = jax.nn.leaky_relu(a_s[src] + a_d[dst], NEG_SLOPE)
            m = jax.ops.segment_max(e, dst, num_segments=n)
            ex = jnp.exp(e - m[dst])
            denom = jax.ops.segment_sum(ex, dst, num_segments=n)
            alpha = ex / denom[dst]
            msg = h[src] * alpha[:, :, None]
            out = jax.ops.segment_sum(msg, dst, num_segments=n)
            return out.reshape(n, HEADS * HID) + b
        key = jax.random.key(seed)
        ks = jax.random.split(key, 12)
        x = jax.random.normal(ks[0], (N, IN_C), dtype=jnp.float32)
        edge_index = jax.random.randint(ks[1], (2, E), 0, N, dtype=jnp.int64)
        s1 = 1.0 / np.sqrt(IN_C)
        W1 = jax.random.normal(ks[2], (IN_C, HEADS * HID), dtype=jnp.float32) * s1
        att_src1 = jax.random.normal(ks[3], (HEADS, HID), dtype=jnp.float32) * 0.1
        att_dst1 = jax.random.normal(ks[4], (HEADS, HID), dtype=jnp.float32) * 0.1
        b1 = jnp.zeros((HEADS * HID,), dtype=jnp.float32)
        s2 = 1.0 / np.sqrt(HEADS * HID)
        W2 = jax.random.normal(ks[5], (HEADS * HID, HEADS * HID), dtype=jnp.float32) * s2
        att_src2 = jax.random.normal(ks[6], (HEADS, HID), dtype=jnp.float32) * 0.1
        att_dst2 = jax.random.normal(ks[7], (HEADS, HID), dtype=jnp.float32) * 0.1
        b2 = jnp.zeros((HEADS * HID,), dtype=jnp.float32)
        return {'x': x, 'edge_index': edge_index, 'W1': W1, 'att_src1': att_src1, 'att_dst1': att_dst1, 'b1': b1, 'W2': W2, 'att_src2': att_src2, 'att_dst2': att_dst2, 'b2': b2}
    _L0_gnn_all = _L0_gnn_setup()
    _L0_gnn_in = {k: v for k, v in _L0_gnn_all.items() if k in ('W1', 'att_src1', 'att_dst1', 'b1', 'W2', 'att_src2', 'att_dst2', 'b2')}
    del _L0_gnn_all

    def _L1_gnn_setup():
        import jax, jax.numpy as jnp
        import numpy as np
        N_NODES = 6250
        N_EDGES = 75000
        C_IN = 256
        C_OUT = 256
        N_REL = 8
        key = jax.random.key(seed)
        ks = jax.random.split(key, 7)
        x = jax.random.normal(ks[0], (N_NODES, C_IN), dtype=jnp.float32)
        edge_index = jax.random.randint(ks[1], (2, N_EDGES), 0, N_NODES, dtype=jnp.int64)
        edge_type = jax.random.randint(ks[2], (N_EDGES,), 0, N_REL, dtype=jnp.int64)
        edge_weight = jax.random.uniform(ks[3], (N_EDGES,), dtype=jnp.float32)
        weight = jax.random.normal(ks[4], (N_REL, C_IN, C_OUT), dtype=jnp.float32) * (1.0 / np.sqrt(C_IN))
        root = jax.random.normal(ks[5], (C_IN, C_OUT), dtype=jnp.float32) * (1.0 / np.sqrt(C_IN))
        bias = jnp.zeros((C_OUT,), dtype=jnp.float32)
        return {'x': x, 'edge_index': edge_index, 'edge_type': edge_type, 'edge_weight': edge_weight, 'weight': weight, 'root': root, 'bias': bias}
    _L1_gnn_all = _L1_gnn_setup()
    _L1_gnn_in = {k: v for k, v in _L1_gnn_all.items() if k in ('weight', 'root', 'bias')}
    del _L1_gnn_all
    return {'x': x, 'src': src, 'dst': dst, 'edge_type_8': edge_type_8, 'edge_weight': edge_weight, 'L0_gnn_W1': _L0_gnn_in['W1'], 'L0_gnn_att_src1': _L0_gnn_in['att_src1'], 'L0_gnn_att_dst1': _L0_gnn_in['att_dst1'], 'L0_gnn_b1': _L0_gnn_in['b1'], 'L0_gnn_W2': _L0_gnn_in['W2'], 'L0_gnn_att_src2': _L0_gnn_in['att_src2'], 'L0_gnn_att_dst2': _L0_gnn_in['att_dst2'], 'L0_gnn_b2': _L0_gnn_in['b2'], 'L1_gnn_weight': _L1_gnn_in['weight'], 'L1_gnn_root': _L1_gnn_in['root'], 'L1_gnn_bias': _L1_gnn_in['bias']}

def reference(x, src, dst, edge_type_8, edge_weight, L0_gnn_W1, L0_gnn_att_src1, L0_gnn_att_dst1, L0_gnn_b1, L0_gnn_W2, L0_gnn_att_src2, L0_gnn_att_dst2, L0_gnn_b2, L1_gnn_weight, L1_gnn_root, L1_gnn_bias):
    import jax
    import jax.numpy as jnp

    def _L0_gnn_ref(x, edge_index, W1, att_src1, att_dst1, b1, W2, att_src2, att_dst2, b2):
        import jax, jax.numpy as jnp
        import numpy as np
        N = 6250
        E = 100000
        IN_C = 256
        HID = 64
        HEADS = 4
        NEG_SLOPE = 0.2

        def _gat_conv(x, W, att_src, att_dst, b, src, dst):
            n = x.shape[0]
            h = (x @ W).reshape(n, HEADS, HID)
            a_s = jnp.einsum('nhc,hc->nh', h, att_src)
            a_d = jnp.einsum('nhc,hc->nh', h, att_dst)
            e = jax.nn.leaky_relu(a_s[src] + a_d[dst], NEG_SLOPE)
            m = jax.ops.segment_max(e, dst, num_segments=n)
            ex = jnp.exp(e - m[dst])
            denom = jax.ops.segment_sum(ex, dst, num_segments=n)
            alpha = ex / denom[dst]
            msg = h[src] * alpha[:, :, None]
            out = jax.ops.segment_sum(msg, dst, num_segments=n)
            return out.reshape(n, HEADS * HID) + b
        loop = jnp.arange(N, dtype=edge_index.dtype)
        src = jnp.concatenate([edge_index[0], loop])
        dst = jnp.concatenate([edge_index[1], loop])
        h = _gat_conv(x, W1, att_src1, att_dst1, b1, src, dst)
        h = jax.nn.elu(h)
        h = _gat_conv(h, W2, att_src2, att_dst2, b2, src, dst)
        h = jax.nn.elu(h)
        return h

    def _L1_gnn_ref(x, edge_index, edge_type, edge_weight, weight, root, bias):
        import jax, jax.numpy as jnp
        import numpy as np
        N_NODES = 6250
        N_EDGES = 75000
        C_IN = 256
        C_OUT = 256
        N_REL = 8
        "RGCNConv (no bases/blocks), aggr='mean', root_weight=True, bias=True.\n\n            Equivalent to the PyG per-relation loop:\n                for r: out += scatter_mean(x[src_r] * w_r, dst_r) @ weight[r]\n                out += x @ root + bias\n            but fused: one segmented mean over (relation, dst) pairs followed by a\n            grouped GEMM over relations.\n            "
        N, C = x.shape
        R = weight.shape[0]
        src, dst = (edge_index[0], edge_index[1])
        msg = x[src] * edge_weight[:, None]
        seg = edge_type * N + dst
        sums = jax.ops.segment_sum(msg, seg, num_segments=R * N)
        cnt = jax.ops.segment_sum(jnp.ones_like(edge_weight), seg, num_segments=R * N)
        h = sums / jnp.maximum(cnt, 1.0)[:, None]
        h = h.reshape(R, N, C)
        out = jnp.einsum('rnc,rco->no', h, weight)
        out = out + x @ root + bias
        return out
    edge_index = jnp.stack([src, dst])
    h = jnp.maximum(_layernorm(x, axis=-1), 0.0)
    x = x + _L0_gnn_ref(h, edge_index, L0_gnn_W1, L0_gnn_att_src1, L0_gnn_att_dst1, L0_gnn_b1, L0_gnn_W2, L0_gnn_att_src2, L0_gnn_att_dst2, L0_gnn_b2)
    h = jnp.maximum(_layernorm(x, axis=-1), 0.0)
    x = x + _L1_gnn_ref(h, edge_index, edge_type_8, edge_weight, L1_gnn_weight, L1_gnn_root, L1_gnn_bias)
    return x

_drawn_inputs = setup_inputs


def setup_inputs(seed=0):
    import zlib

    import numpy as np

    out = dict(_drawn_inputs(seed))
    spreads = {'L0_gnn_b1': (0.0, 0.1), 'L0_gnn_b2': (0.0, 0.1), 'L1_gnn_bias': (0.0, 0.1)}
    factors = {'L0_gnn_att_src1': 2.744,
     'L0_gnn_att_dst1': 8.0,
     'L0_gnn_att_src2': 8.0,
     'L0_gnn_att_dst2': 8.0}
    for name, (base, spread) in spreads.items():
        noise = np.random.default_rng([zlib.crc32(name.encode()), seed]).standard_normal(out[name].shape)
        drawn = base * np.exp(spread * noise) if base else spread * noise
        out[name] = jnp.asarray(drawn.astype(out[name].dtype))
    for name, factor in factors.items():
        out[name] = (out[name] * factor).astype(out[name].dtype)
    return out
```

```python
import concourse.bass as bass
from concourse import mybir
from contextlib import ExitStack

F32 = mybir.dt.float32
BF16 = mybir.dt.bfloat16
I32 = mybir.dt.int32
ALU = mybir.AluOpType
ACT = mybir.ActivationFunctionType
AX = mybir.AxisListType

P = 128
N_NODES = 12500
N_EDGES = 212500
N_LOOPED = 6250
D = 256
HEADS = 4
HID = 64
N_REL = 8
SLOPE = 0.2
EPS = 1e-5
BIG = 1e30
TINY = 1e-30

TILES = 13
CHUNK = TILES * P
N_CHUNKS = -(-N_EDGES // CHUNK)
NODE_TILES = N_NODES // P + 2
NP = NODE_TILES * P
NODE_SLOTS = 3
NODE_TURNS = NODE_TILES // NODE_SLOTS
MAX_STEPS = N_CHUNKS + NODE_TILES + 5
PAD_KEY = 1 << 20
KEYS = TILES + 2
RECORD = KEYS + 2 * TILES

TABLE = D + 2 * HEADS
ES, MS, RS = D, D + HEADS, D + 2 * HEADS
WIDE = TABLE + N_REL


class Turn:

    def __init__(self, engine, sem, per_turn, turn):
        self.engine, self.sem, self.per_turn, self.turn, self.count = engine, sem, per_turn, turn, 0

    def add(self, instruction):
        instruction.then_inc(self.sem, 1)
        self.count += 1

    def settle(self):
        self.engine.wait_ge(self.sem, self.turn * self.per_turn + self.count)

    def end(self):
        assert self.count == self.per_turn, (self.count, self.per_turn)


def build(nc, x, records, firsts, lasts, ewt, W1, as1, ad1, b1, W2, as2, ad2, b2, Wr, root, rbias, out):
    assert N_CHUNKS == P and NODE_TILES % NODE_SLOTS == 0

    def dram(name, shape, dt):
        return nc.dram_tensor(name, shape, dt, kind="Internal").ap()

    tables = [dram("node_rows_1", (NP, TABLE), F32), dram("node_rows_2", (NP, TABLE), F32)]
    ads = [dram("a_dst_parts_1", (NP, 3 * HEADS), BF16), dram("a_dst_parts_2", (NP, 3 * HEADS), BF16)]
    accs = [dram("edge_sums_1", (NP, WIDE), F32), dram("edge_sums_2", (NP, WIDE), F32)]
    icd = dram("inverse_count_parts", (NP, 3 * N_REL), BF16)
    yrel = dram("relation_rows", (NP, N_REL * D), F32)
    rootd = dram("root_rows", (NP, D), F32)
    yrows = yrel.rearrange("n (r d) -> (n r) d", r=N_REL)

    ctx = ExitStack()
    with ctx:
        def sb(name, shape, dt=F32):
            return ctx.enter_context(nc.sbuf_tensor(name, shape, dt))

        def sem(name):
            return ctx.enter_context(nc.semaphore(name))

        bank = [ctx.enter_context(nc.psum_tensor(f"bank{i}", [P, 512], F32)) for i in range(8)]

        ident = sb("ident", [P, P])
        identb = sb("identb", [P, P], BF16)
        ones = sb("ones", [P, P])
        iota_win = sb("iota_win", [P, P])
        iota_part = sb("iota_part", [P, 1])
        iota_steps = sb("iota_steps", [P, MAX_STEPS])
        iota_rel = sb("iota_rel", [P, N_REL])
        eps_t = sb("eps_t", [P, 1])
        head_rows = sb("head_rows", [HEADS + 1, WIDE])
        first_row = sb("first_row", [1, P])
        node_no = sb("node_no", [P, NODE_TILES])
        looped = sb("looped", [P, NODE_TILES])
        loop_bias = sb("loop_bias", [P, NODE_TILES])

        ends_i = sb("ends_i", [1, 2, P], I32)
        ends = sb("ends", [1, 2, P])
        plan = sb("plan", [1, 6, P])
        plan_i = sb("plan_i", [1, P], I32)
        cols = sb("cols", [P, 3])
        hot = sb("hot", [P, 4, MAX_STEPS])
        base_of = sb("base_of", [P, MAX_STEPS + 1])
        step_i = sb("step_i", [1, 2, MAX_STEPS], I32)
        turns_i = sb("turns_i", [1, 2], I32)

        wx = [sb("w1x", [P, 2, TABLE]), sb("w2x", [P, 2, TABLE])]
        att = sb("att", [P, 4, D])
        att_tmp = sb("att_tmp", [P, 2, D])
        biases = sb("biases", [P, 3, D])
        wrel = sb("wrel", [P, 2, N_REL + 1, D])

        KN = NODE_SLOTS
        n_x = sb("n_x", [P, KN, D])
        n_own = sb("n_own", [P, KN, TABLE])
        n_acc = sb("n_acc", [P, KN, WIDE])
        n_st = sb("n_st", [P, KN, 16])
        n_h = sb("n_h", [P, KN, D])
        n_t = sb("n_t", [P, KN, D])
        n_hT = sb("n_hT", [P, KN, 2, P])
        n_out = sb("n_out", [P, KN, TABLE])
        n_y = sb("n_y", [P, KN, N_REL * D])
        n_par = sb("n_par", [P, KN, 3 * N_REL], BF16)
        n_adp = sb("n_adp", [P, KN, 3 * HEADS], BF16)
        n_sm = sb("n_sm", [P, KN, 64])

        record = sb("record", [P, 2, RECORD], I32)
        key_i = record[:, :, 0:KEYS]
        src_i = record[:, :, KEYS:KEYS + TILES]
        typ_i = record[:, :, KEYS + TILES:RECORD]
        row_i = sb("row_i", [P, 2, TILES], I32)
        wts = sb("wts", [P, 2, TILES])
        keyf = sb("keyf", [P, 2, KEYS])
        win_ad = sb("win_ad", [P, 2, 3 * HEADS], BF16)
        win_ic = sb("win_ic", [P, 2, 3 * N_REL], BF16)
        win_root = sb("win_root", [P, 2, D])
        rows = sb("rows", [P, 2, TILES, WIDE])
        onehot = sb("onehot", [P, 2, TILES, P])
        onehot_b = sb("onehot_b", [P, TILES, P], BF16)
        onehot_T = sb("onehot_T", [P, TILES, P], BF16)
        differ = sb("differ", [P, 2, TILES + 1])
        cut = sb("cut", [P, 2, HEADS * (TILES + 1) + 1])
        sc = sb("sc", [P, HEADS * (TILES + 1)])
        run_f = sb("run_f", [P, HEADS * (TILES + 1)])
        run_m = sb("run_m", [P, HEADS * (TILES + 1)])
        tmp_m = sb("tmp_m", [P, HEADS * (TILES + 1)])
        z = sb("z", [P, TILES, HEADS])
        zz = sb("zz", [P, HEADS, TILES])
        not_first = sb("not_first", [P, 2, TILES])
        not_final = sb("not_final", [P, 2, TILES])
        edge_ends = sb("edge_ends", [P, 2, P])
        seq_v = sb("seq_v", [HEADS, 2 * P])
        seq_c = sb("seq_c", [HEADS, 2 * P + 1])
        seq_f = sb("seq_f", [HEADS, 2, 2 * P])
        seq_m = sb("seq_m", [HEADS, 2 * P])
        fac_d = sb("fac_d", [HEADS, 1])
        fac = sb("fac", [HEADS + 1, 1])
        fac_row = sb("fac_row", [1, WIDE])
        carry = sb("carry", [1, WIDE])
        sel = sb("sel", [P, 2])
        acc_sb = sb("acc_sb", [P, 2, WIDE])
        out_sb = sb("out_sb", [P, 2, D])
        typ_hot = sb("typ_hot", [P, TILES, N_REL])
        ic = sb("ic", [P, TILES, N_REL])
        coef = sb("coef", [P, TILES])
        zeros_t = sb("zeros_t", [P, WIDE])

        s_const = sem("s_const")
        s_wload = sem("s_wload")
        s_vplan = sem("s_vplan")
        s_plan_row = sem("s_plan_row")
        s_plan_col = sem("s_plan_col")
        s_plan_hot = sem("s_plan_hot")
        s_plan_sum = sem("s_plan_sum")
        s_plan = sem("s_plan")
        s_zeroed = sem("s_zeroed")
        s_pool = sem("s_pool")
        s_passed = sem("s_passed")

        class NodeSems:

            def __init__(self, n):
                self.loaded = [sem(f"n{n}_loaded{k}") for k in range(NODE_SLOTS)]
                self.stored = [sem(f"n{n}_stored{k}") for k in range(NODE_SLOTS)]
                self.vec = sem(f"n{n}_vec")
                if n > 0:
                    self.dist = sem(f"n{n}_dist")
                    self.wexp = sem(f"n{n}_wexp")
                    self.neg = sem(f"n{n}_neg")
                    self.negexp = sem(f"n{n}_negexp")
                if n != 1:
                    self.var = sem(f"n{n}_var")
                    self.std = sem(f"n{n}_std")
                self.h = sem(f"n{n}_h")
                self.hT = sem(f"n{n}_hT")
                self.hTs = sem(f"n{n}_hTs")
                self.mm = sem(f"n{n}_mm")
                self.res = sem(f"n{n}_res")
                if n == 2:
                    self.copied = sem("n2_copied")

        class EdgeSems:

            def __init__(self, n):
                self.loaded = [sem(f"e{n}_loaded{u}") for u in range(2)]
                self.gathered = [sem(f"e{n}_gathered{u}") for u in range(2)]
                self.stored = sem(f"e{n}_stored")
                self.vec = sem(f"e{n}_vec")
                self.hot = sem(f"e{n}_hot")
                self.hotb = sem(f"e{n}_hotb")
                self.hotT = sem(f"e{n}_hotT")
                self.hotTs = sem(f"e{n}_hotTs")
                self.dstv = sem(f"e{n}_dstv")
                self.sel = sem(f"e{n}_sel")
                self.pick = sem(f"e{n}_pick")
                self.carry = sem(f"e{n}_carry")
                self.rhs = sem(f"e{n}_rhs")
                self.done = sem(f"e{n}_done")
                self.acc = sem(f"e{n}_acc")
                if n < 2:
                    self.ends = sem(f"e{n}_ends")
                    self.endsT = sem(f"e{n}_endsT")
                    self.seq = sem(f"e{n}_seq")
                    self.seqm = sem(f"e{n}_seqm")
                    self.back = sem(f"e{n}_back")
                    self.facd = sem(f"e{n}_facd")
                    self.fac = sem(f"e{n}_fac")
                    self.facr = sem(f"e{n}_facr")
                    self.expd = sem(f"e{n}_expd")
                    self.exp = sem(f"e{n}_exp")
                else:
                    self.idx = sem(f"e{n}_idx")
                    self.outw = sem(f"e{n}_outw")

        ns = [NodeSems(n) for n in range(3)]
        es = [EdgeSems(n) for n in range(3)]

        block = ctx.enter_context(nc.Block())

        def by_head(t, n=TILES + 1, part=P):
            return t.rearrange("p (h t) -> p h t", h=HEADS)

        x_v = x.rearrange("(j p) d -> j p d", p=P)

        n_stores = (2, 3, 2)
        edge_loads_per_step = (2, 2, 4)
        width = (WIDE, TABLE, D)

        def tile_rows(ap, j):
            return ap[bass.ds(j * P, P), :]

        @block.sync
        def _(sp):
            sp.dma_start(ends_i[0:1, 0, :], firsts).then_inc(s_wload, 16)
            sp.dma_start(ends_i[0:1, 1, :], lasts).then_inc(s_wload, 16)
            for t, W in ((wx[0], W1), (wx[1], W2)):
                sp.dma_start(t[:, :, 0:D], W.rearrange("(k p) n -> p k n", p=P)).then_inc(s_wload, 16)
            for q, a in enumerate((as1, ad1, as2, ad2)):
                sp.dma_start(att[:, q, :], a.rearrange("h d -> (h d)").partition_broadcast(P)).then_inc(s_wload, 16)
            for q, b in enumerate((b1, b2, rbias)):
                sp.dma_start(biases[:, q, :], b.partition_broadcast(P)).then_inc(s_wload, 16)
            for r in range(N_REL):
                sp.dma_start(wrel[:, :, r, :], Wr[r].rearrange("(k p) n -> p k n", p=P)).then_inc(s_wload, 16)
            sp.dma_start(wrel[:, :, N_REL, :], root.rearrange("(k p) n -> p k n", p=P)).then_inc(s_wload, 16)
            sp.wait_ge(s_const, 1)
            for a in accs:
                for j in (NODE_TILES - 2, NODE_TILES - 1):
                    sp.dma_start(a[j * P:(j + 1) * P, :], zeros_t[:, :]).then_inc(s_zeroed, 16)
            sp.wait_ge(s_zeroed, 64)
            sp.wait_ge(s_plan, 1)
            turns = nc.sync.value_load(turns_i[0:1, 1:2], min_val=1, max_val=MAX_STEPS // 2)

            def node_loads(n):
                s = ns[n]
                with sp.Fori(0, NODE_TURNS) as i:
                    for k in range(NODE_SLOTS):
                        sp.wait_ge(s.stored[k], i * (16 * n_stores[n]) + 16)
                        j = i * NODE_SLOTS + k
                        if n != 1:
                            sp.dma_start(n_x[:, k, :], tile_rows(x, j)).then_inc(s.loaded[k], 16)
                        if n > 0:
                            sp.dma_start(n_acc[:, k, 0:width[n - 1]], accs[n - 1][bass.ds(j * P, P), 0:width[n - 1]]).then_inc(s.loaded[k], 16)
                            sp.dma_start(n_own[:, k, :], tile_rows(tables[n - 1], j)).then_inc(s.loaded[k], 16)

            def edge_loads(n):
                s = es[n]
                with sp.Fori(0, turns) as i:
                    for u in range(2):
                        step = i * 2 + u
                        r0 = nc.sync.value_load(step_i[0:1, 0, bass.ds(step, 1)], min_val=0, max_val=N_CHUNKS * P)
                        b0 = nc.sync.value_load(step_i[0:1, 1, bass.ds(step, 1)], min_val=0, max_val=N_NODES)
                        sp.wait_ge(s.done, i * 2 + (u + 1))
                        if n == 2:
                            sp.wait_ge(s.outw, i * 2 + (u + 1))
                        sp.dma_start(record[:, u, :], records[bass.ds(r0, P), :]).then_inc(s.loaded[u], 16)
                        if n < 2:
                            sp.dma_start(win_ad[:, u, :], ads[n][bass.ds(b0, P), :]).then_inc(s.loaded[u], 16)
                        else:
                            sp.dma_start(wts[:, u, :], ewt[bass.ds(r0, P), :]).then_inc(s.loaded[u], 16)
                            sp.dma_start(win_ic[:, u, :], icd[bass.ds(b0, P), :]).then_inc(s.loaded[u], 16)
                            sp.dma_start(win_root[:, u, :], rootd[bass.ds(b0, P), :]).then_inc(s.loaded[u], 16)

            for n in range(3):
                node_loads(n)
                for k in range(NODE_SLOTS):
                    sp.wait_ge(ns[n].stored[k], 16 + NODE_TURNS * 16 * n_stores[n])
                edge_loads(n)
                sp.wait_ge(es[n].stored, turns * 32 + 16)
                sp.sem_inc(s_passed, 1)


        @block.gpsimd
        def _(pool):
            g = nc.gpsimd
            g.memset(ident[:], 0.0)
            g.memset(identb[:], 0.0)
            g.memset(ones[:], 1.0)
            g.memset(eps_t[:], EPS)
            g.memset(zeros_t[:], 0.0)
            g.memset(acc_sb[:], 0.0)
            g.memset(edge_ends[:], 0.0)
            g.memset(cut[:], -BIG)
            g.memset(sc[:], -BIG)
            g.memset(seq_c[:], 0.0)
            g.memset(seq_f[:], -BIG)
            g.memset(fac[:], 1.0)
            g.memset(first_row[:], 0.0)
            g.memset(base_of[:], -4.0 * PAD_KEY)
            g.memset(head_rows[:], 0.0)
            g.iota(iota_win[:], [[1, P]], base=0, channel_multiplier=0, allow_small_or_imprecise_dtypes=True)
            g.iota(iota_part[:], [[0, 1]], base=0, channel_multiplier=1, allow_small_or_imprecise_dtypes=True)
            g.iota(iota_steps[:], [[1, MAX_STEPS]], base=0, channel_multiplier=0, allow_small_or_imprecise_dtypes=True)
            g.iota(iota_rel[:], [[1, N_REL]], base=0, channel_multiplier=0, allow_small_or_imprecise_dtypes=True)
            g.iota(node_no[:], [[P, NODE_TILES]], base=0, channel_multiplier=1,
                   allow_small_or_imprecise_dtypes=True).then_inc(s_pool, 1)
            pool.wait_ge(s_pool, 1)
            g.memset(first_row[0:1, 0:1], 1.0)
            g.affine_select(out=ident[:], in_=ident[:], compare_op=ALU.not_equal, fill=1.0, base=0,
                            pattern=[[-1, P]], channel_multiplier=1)
            g.affine_select(out=identb[:], in_=identb[:], compare_op=ALU.not_equal, fill=1.0, base=0,
                            pattern=[[-1, P]], channel_multiplier=1)
            g.affine_select(out=head_rows[:, 0:D], in_=head_rows[:, 0:D], compare_op=ALU.not_equal, fill=1.0, base=0,
                            pattern=[[-1, HEADS], [0, HID]], channel_multiplier=1)
            g.affine_select(out=head_rows[:, ES:MS], in_=head_rows[:, ES:MS], compare_op=ALU.not_equal, fill=1.0,
                            base=0, pattern=[[-1, HEADS]], channel_multiplier=1)
            g.affine_select(out=head_rows[:, RS:WIDE], in_=head_rows[:, RS:WIDE], compare_op=ALU.not_equal, fill=1.0,
                            base=-HEADS, pattern=[[0, N_REL]], channel_multiplier=1)
            g.tensor_scalar(looped[:], node_no[:], float(N_LOOPED), None, ALU.is_lt).then_inc(s_pool, 1)
            pool.wait_ge(s_pool, 2)
            g.tensor_scalar(loop_bias[:], looped[:], -1.0, BIG, ALU.add, ALU.mult).then_inc(s_const, 1)

            pool.wait_ge(s_plan, 1)
            turns = g.value_load(turns_i[0:1, 1:2], min_val=1, max_val=MAX_STEPS // 2)

            def gathers(n):
                s = es[n]
                with pool.Fori(0, turns) as i:
                    for u in range(2):
                        if n < 2:
                            pool.wait_ge(s.loaded[u], (i + 1) * (16 * edge_loads_per_step[n]))
                        else:
                            pool.wait_ge(s.idx, i * 2 + (u + 1))
                        pool.sem_inc(s_passed, 1)
                        for t in range(TILES):
                            if n < 2:
                                g.indirect_dma_start(
                                    out=rows[:, u, t, 0:TABLE], out_offset=None, in_=tables[n][:, :],
                                    in_offset=bass.IndirectOffsetOnAxis(ap=src_i[:, u, t:t + 1], axis=0),
                                ).then_inc(s.gathered[u], 16)
                            else:
                                g.indirect_dma_start(
                                    out=rows[:, u, t, 0:D], out_offset=None, in_=yrows[:, :],
                                    in_offset=bass.IndirectOffsetOnAxis(ap=row_i[:, u, t:t + 1], axis=0),
                                ).then_inc(s.gathered[u], 16)

            for n in range(3):
                gathers(n)

        @block.scalar
        def _(act):
            a = nc.scalar
            for n in range(3):
                for k in range(NODE_SLOTS):
                    act.sem_inc(ns[n].stored[k], 16)
            act.wait_ge(s_plan, 1)
            turns = a.value_load(turns_i[0:1, 1:2], min_val=1, max_val=MAX_STEPS // 2)

            def node_act(n):
                s = ns[n]
                with act.Fori(0, NODE_TURNS) as i:
                    for k in range(NODE_SLOTS):
                        j = i * NODE_SLOTS + k
                        if n > 0:
                            act.wait_ge(s.dist, j + 1)
                            a.activation(n_sm[:, k, 8:16], n_sm[:, k, 0:8], ACT.Exp).then_inc(s.wexp, 1)
                            act.wait_ge(s.neg, j + 1)
                            a.activation(n_h[:, k, :], n_t[:, k, :], ACT.Exp).then_inc(s.negexp, 1)
                        if n != 1:
                            act.wait_ge(s.var, j + 1)
                            a.activation(n_st[:, k, 8:9], n_st[:, k, 7:8], ACT.Sqrt, bias=eps_t[:, 0:1]).then_inc(s.std, 1)
                        act.wait_ge(s.hT, j + 1)
                        f = ACT.Copy if n == 1 else ACT.Relu
                        a.activation(n_hT[:, k, :, :], bank[0][:, 0:D].rearrange("p (c q) -> p c q", c=2), f).then_inc(s.hTs, 1)
                        if n == 2:
                            act.wait_ge(s.stored[k], i * 32 + 16)
                            for q in range(4):
                                act.wait_ge(s.mm, j * 5 + (q + 1))
                                a.activation(n_y[:, k, q * 512:(q + 1) * 512], bank[2 + q][:, :], ACT.Copy).then_inc(s.copied, 1)
                            act.wait_ge(s.copied, (j + 2) * 4)
                            act.dma_start(tile_rows(yrel, j), n_y[:, k, :]).then_inc(s.stored[k], 16)
                            act.wait_ge(s.res, j + 2)
                            act.dma_start(tile_rows(rootd, j), n_out[:, k, 0:D]).then_inc(s.stored[k], 16)
                        else:
                            act.wait_ge(s.res, j + 2)
                            act.dma_start(tile_rows(tables[n], j), n_out[:, k, :]).then_inc(s.stored[k], 16)
                            act.dma_start(tile_rows(ads[n], j), n_adp[:, k, :]).then_inc(s.stored[k], 16)
                            if n == 1:
                                act.dma_start(tile_rows(icd, j), n_par[:, k, :]).then_inc(s.stored[k], 16)

            def edge_act(n):
                s = es[n]
                w = width[n]
                with act.Fori(0, turns) as i:
                    for u in range(2):
                        step = i * 2 + u
                        b0 = a.value_load(step_i[0:1, 1, bass.ds(step, 1)], min_val=0, max_val=N_NODES)
                        act.wait_ge(s.hot, step + 1)
                        a.activation(onehot_b[:], onehot[:, u, :, :], ACT.Copy).then_inc(s.hotb, 1)
                        act.wait_ge(s.hotT, step + 1)
                        for half, (t0, t1) in enumerate(((0, 7), (7, TILES))):
                            last = a.activation(onehot_T[:, t0:t1, :],
                                                bank[half].bitcast(BF16)[:, 0:(t1 - t0) * P].rearrange("p (t m) -> p t m", m=P), ACT.Copy)
                        last.then_inc(s.hotTs, 1)
                        if n < 2:
                            act.wait_ge(s.endsT, step + 1)
                            a.activation(seq_v[:, 0::2], bank[3][0:HEADS, 0:P], ACT.Copy)
                            a.activation(seq_v[:, 1::2], bank[3][32:32 + HEADS, 0:P], ACT.Copy)
                            a.activation(seq_c[:, 0:2 * P:2], bank[3][64:64 + HEADS, 0:P], ACT.Copy)
                            a.activation(seq_c[:, 1:2 * P:2], bank[3][96:96 + HEADS, 0:P], ACT.Copy).then_inc(s.seq, 1)
                            act.wait_ge(s.facd, step + 1)
                            a.activation(fac[0:HEADS, :], fac_d[:, :], ACT.Exp).then_inc(s.fac, 1)
                            act.wait_ge(s.expd, step + 1)
                            a.activation(rows[:, u, :, ES:MS], zz.rearrange("p h t -> p t h"), ACT.Exp).then_inc(s.exp, 1)
                            act.wait_ge(s.pick, step + 1)
                            a.activation(fac_row[:, 0:w], bank[3][0:1, 0:w], ACT.Copy).then_inc(s.facr, 1)
                        act.wait_ge(s.done, step + 3)
                        a.activation(acc_sb[:, u, 0:w], bank[6 + u][:, 0:w], ACT.Copy).then_inc(s.acc, 1)
                        act.wait_ge(s.stored, step * 16 + 16)
                        if n < 2:
                            act.wait_ge(s.acc, step + 2)
                            act.dma_start(accs[n][bass.ds(b0, P), 0:w], acc_sb[:, u, 0:w]).then_inc(s.stored, 16)
                        else:
                            act.wait_ge(s.outw, step + 3)
                            act.dma_start(out[bass.ds(b0, P), :], out_sb[:, u, :]).then_inc(s.stored, 16)

            for n in range(3):
                node_act(n)
                act.sem_inc(es[n].stored, 16)
                edge_act(n)

        @block.tensor
        def _(pe):
            t_ = nc.tensor
            for n in range(3):
                pe.sem_inc(es[n].done, 2)
            pe.wait_ge(s_const, 1)
            pe.wait_ge(s_plan_row, 1)
            for q, row in enumerate((3, 4, 5)):
                last = t_.matmul(bank[0][:, q:q + 1], plan[0:1, row, :], ones[0:1, 0:1], start=True, stop=True)
            last.then_inc(s_plan_col, 1)
            pe.wait_ge(s_plan_hot, 1)
            for q, m in enumerate((0, 2, 3)):
                last = t_.matmul(bank[1 + q][:, 0:MAX_STEPS], ones[:, :], hot[:, m, :], start=True, stop=True)
            last.then_inc(s_plan_sum, 1)
            pe.wait_ge(s_plan, 1)
            turns = t_.value_load(turns_i[0:1, 1:2], min_val=1, max_val=MAX_STEPS // 2)

            def node_pe(n):
                s = ns[n]
                with pe.Fori(0, NODE_TURNS) as i:
                    for k in range(NODE_SLOTS):
                        j = i * NODE_SLOTS + k
                        pe.wait_ge(s.h, j + 1)
                        pe.wait_ge(s.hTs, j + 1)
                        for c in range(2):
                            last = t_.transpose(bank[0][:, c * P:(c + 1) * P], n_h[:, k, c * P:(c + 1) * P], ident[:])
                        last.then_inc(s.hT, 1)
                        pe.wait_ge(s.hTs, j + 2)
                        pe.wait_ge(s.res, j + 1)
                        if n < 2:
                            for c in range(2):
                                last = t_.matmul(bank[1][:, 0:TABLE], n_hT[:, k, c, :], wx[n][:, c, :], start=(c == 0), stop=(c == 1))
                            last.then_inc(s.mm, 1)
                        else:
                            pe.wait_ge(s.copied, j * 4 + 4)
                            for q in range(5):
                                w = 2 if q < 4 else 1
                                for c in range(2):
                                    last = t_.matmul(bank[2 + q][:, 0:w * D], n_hT[:, k, c, :],
                                                     wrel[:, c, 2 * q:2 * q + w, :], start=(c == 0), stop=(c == 1))
                                last.then_inc(s.mm, 1)

            def edge_pe(n):
                s = es[n]
                w = width[n]
                with pe.Fori(0, turns) as i:
                    for u in range(2):
                        step = i * 2 + u
                        pe.wait_ge(s.hotb, step + 1)
                        for t in range(TILES):
                            b, o = (0, t) if t < 7 else (1, t - 7)
                            last = t_.transpose(bank[b].bitcast(BF16)[:, o * P:(o + 1) * P], onehot_b[:, t, :], identb[:])
                        last.then_inc(s.hotT, 1)
                        pe.wait_ge(s.hotTs, step + 1)
                        nv = 3 * HEADS if n < 2 else 3 * N_REL
                        win = win_ad if n < 2 else win_ic
                        for t in range(TILES):
                            last = t_.matmul(bank[2][:, t * nv:(t + 1) * nv], onehot_T[:, t, :], win[:, u, :], start=True, stop=True)
                        last.then_inc(s.dstv, 1)
                        if n < 2:
                            pe.wait_ge(s.ends, step + 1)
                            t_.transpose(bank[3][:, 0:P], edge_ends[:, u, :], ident[:]).then_inc(s.endsT, 1)
                            pe.wait_ge(s.seqm, step + 1)
                            pe.sem_inc(s_passed, 1)
                            t_.transpose(bank[5][:, 0:HEADS], seq_m[:, 0::2], ident[0:HEADS, 0:HEADS])
                            t_.transpose(bank[5][:, HEADS:2 * HEADS], seq_m[:, 1::2], ident[0:HEADS, 0:HEADS]).then_inc(s.back, 1)
                            pe.wait_ge(s.fac, step + 1)
                            pe.sem_inc(s_passed, 1)
                            t_.matmul(bank[3][0:1, 0:w], fac[:, :], head_rows[:, 0:w], start=True, stop=True)
                        pe.wait_ge(s.sel, step + 1)
                        pe.wait_ge(s.acc, step + 1)
                        if n == 2:
                            pe.wait_ge(s.outw, step + 1)
                        t_.matmul(bank[4][0:1, 0:w], sel[:, u:u + 1], acc_sb[:, 1 - u, 0:w], start=True, stop=True).then_inc(s.pick, 1)
                        for half, (t0, t1) in enumerate(((0, 7), (7, TILES))):
                            pe.wait_ge(s.rhs, step * 2 + (half + 1))
                            for t in range(t0, t1):
                                t_.matmul(bank[6 + u][:, 0:w], onehot[:, u, t, :], rows[:, u, t, 0:w], start=(t == 0), stop=False)
                        pe.wait_ge(s.carry, step + 1)
                        t_.matmul(bank[6 + u][:, 0:w], first_row[0:1, :], carry[0:1, 0:w], start=False, stop=True).then_inc(s.done, 1)

            for n in range(3):
                node_pe(n)
                edge_pe(n)

        @block.vector
        def _(dve):
            v = nc.vector
            for n in range(3):
                dve.sem_inc(ns[n].res, 1)
                dve.sem_inc(es[n].acc, 1)
                dve.sem_inc(ns[n].hTs, 1)
            dve.sem_inc(ns[2].copied, 4)
            dve.sem_inc(es[2].outw, 2)
            dve.wait_ge(s_const, 1)
            dve.wait_ge(s_wload, 16 * 20)
            nwork = [0]

            def do(ins):
                nwork[0] += 1
                ins.then_inc(s_vplan, 1)
                dve.wait_ge(s_vplan, nwork[0])

            B, E_, NW, CUM, CUX, V = range(6)
            do(v.tensor_copy(ends[:], ends_i[:]))
            do(v.memset(ends[0:1, 0, 0:1], 0.0))
            do(v.tensor_copy(plan[0:1, B, :], ends[0:1, 0, :]))
            do(v.tensor_scalar(plan[0:1, E_, 0:P - 1], ends[0:1, 0, 1:P], -1.0, None, ALU.add))
            do(v.memset(plan[0:1, E_, P - 1:P], float(N_NODES - 1)))
            do(v.tensor_scalar(ends[0:1, 1, :], ends[0:1, 1, :], float(N_NODES - 1), None, ALU.min))
            do(v.tensor_tensor(plan[0:1, E_, :], plan[0:1, E_, :], ends[0:1, 1, :], ALU.max))
            do(v.tensor_tensor(plan_i[0:1, :], plan[0:1, E_, :], plan[0:1, B, :], ALU.subtract))
            do(v.tensor_scalar(plan_i[0:1, :], plan_i[0:1, :], 7, None, ALU.arith_shift_right))
            do(v.tensor_copy(plan[0:1, NW, :], plan_i[0:1, :]))
            do(v.tensor_scalar(plan[0:1, NW, :], plan[0:1, NW, :], 1.0, None, ALU.add))
            do(v.tensor_tensor_scan(plan[0:1, CUM, :], plan[0:1, NW, :], zeros_t[0:1, 0:P], 0.0, ALU.add, ALU.add))
            do(v.tensor_tensor(plan[0:1, CUX, :], plan[0:1, CUM, :], plan[0:1, NW, :], ALU.subtract))
            do(v.tensor_scalar(plan[0:1, V, 0:1], plan[0:1, CUM, P - 1:P], 1.0, None, ALU.add))
            do(v.tensor_copy(turns_i[0:1, 0:1], plan[0:1, V, 0:1]))
            do(v.tensor_scalar(turns_i[0:1, 1:2], turns_i[0:1, 0:1], 1, None, ALU.arith_shift_right))
            v.scalar_tensor_tensor(plan[0:1, V, :], plan[0:1, CUX, :], -float(P), plan[0:1, B, :], ALU.mult, ALU.add).then_inc(s_plan_row, 1)
            dve.wait_ge(s_plan_col, 1)
            do(v.tensor_copy(cols[:], bank[0][:, 0:3]))
            do(v.tensor_scalar(hot[:, 0, :], iota_steps[:], cols[:, 0:1], None, ALU.is_ge))
            do(v.tensor_scalar(hot[:, 1, :], iota_steps[:], cols[:, 1:2], None, ALU.is_ge))
            do(v.tensor_tensor(hot[:, 2, :], hot[:, 1, :], hot[:, 0, :], ALU.subtract))
            v.tensor_scalar(hot[:, 3, :], hot[:, 2, :], cols[:, 2:3], None, ALU.mult).then_inc(s_plan_hot, 1)
            dve.wait_ge(s_plan_sum, 1)
            do(v.tensor_scalar(hot[:, 0, :], iota_steps[:], float(P), -float(N_NODES), ALU.mult, ALU.add))
            do(v.tensor_tensor(hot[:, 0, :], hot[:, 0, :], bank[2][:, 0:MAX_STEPS], ALU.mult))
            do(v.tensor_tensor(hot[:, 0, :], hot[:, 0, :], bank[3][:, 0:MAX_STEPS], ALU.add))
            do(v.tensor_scalar(base_of[:, 1:MAX_STEPS + 1], hot[:, 0, :], float(N_NODES), None, ALU.add))
            do(v.tensor_scalar(step_i[0:1, 0, :], bank[1][0:1, 0:MAX_STEPS], float(P), None, ALU.mult))
            for n in range(2):
                for q in range(2):
                    a_ = att[:, 2 * n + q, :].unsqueeze(1).to_broadcast([P, 2, D])
                    do(v.tensor_tensor(att_tmp[:], wx[n][:, :, 0:D], a_, ALU.mult))
                    do(v.tensor_reduce(wx[n][:, :, D + q * HEADS:D + (q + 1) * HEADS],
                                       att_tmp.rearrange("p k (h d) -> p k h d", h=HEADS), AX.X, ALU.add))
            v.tensor_copy(step_i[0:1, 1, :], base_of[0:1, 1:MAX_STEPS + 1]).then_inc(s_plan, 1)
            dve.wait_ge(s_plan, 1)
            turns = v.value_load(turns_i[0:1, 1:2], min_val=1, max_val=MAX_STEPS // 2)

            def split(t, parts, value, rest, signal=None):
                t.add(v.tensor_copy(parts[:, :, 0], value))
                t.settle()
                t.add(v.tensor_tensor(rest, value, parts[:, :, 0], ALU.subtract))
                t.settle()
                t.add(v.tensor_copy(parts[:, :, 1], rest))
                t.settle()
                t.add(v.tensor_tensor(rest, rest, parts[:, :, 1], ALU.subtract))
                t.settle()
                if signal is None:
                    t.add(v.tensor_copy(parts[:, :, 2], rest))
                else:
                    v.tensor_copy(parts[:, :, 2], rest).then_inc(signal, 1)

            def head_bcast(ap):
                return ap.unsqueeze(2).to_broadcast([P, HEADS, HID])

            def heads(ap):
                return ap.rearrange("p (h d) -> p h d", h=HEADS)

            def node_vec(n):
                s = ns[n]
                n_loads = (1, 2, 3)[n]
                per = (7, 31, 23)[n]
                with dve.Fori(0, NODE_TURNS) as i:
                    for k in range(NODE_SLOTS):
                        j = i * NODE_SLOTS + k
                        t = Turn(dve, s.vec, per, j)
                        sm, own, acc, tmp, h = n_sm[:, k, :], n_own[:, k, :], n_acc[:, k, :], n_t[:, k, :], n_h[:, k, :]
                        xin = n_x[:, k, :]
                        dve.wait_ge(s.loaded[k], (i + 1) * (16 * n_loads))

                        def go(ins):
                            t.add(ins)
                            t.settle()

                        if n > 0:
                            e, m, den = sm[:, 16:20], sm[:, 20:24], sm[:, 24:28]
                            go(v.tensor_tensor(e, own[:, D:D + HEADS], own[:, D + HEADS:TABLE], ALU.add))
                            go(v.scalar_tensor_tensor(e, e, SLOPE, e, ALU.mult, ALU.max))
                            go(v.tensor_scalar(e, e, loop_bias[:, bass.ds(j, 1)], None, ALU.add))
                            go(v.tensor_scalar(m, acc[:, ES:MS], 0.0, -BIG, ALU.is_le, ALU.mult))
                            go(v.tensor_tensor(m, m, acc[:, MS:RS], ALU.add))
                            go(v.tensor_tensor(den, m, e, ALU.max))
                            t.add(v.tensor_tensor(sm[:, 0:4], m, den, ALU.subtract))
                            v.tensor_tensor(sm[:, 4:8], e, den, ALU.subtract).then_inc(s.dist, 1)
                            dve.wait_ge(s.wexp, j + 1)
                            go(v.tensor_scalar(sm[:, 12:16], sm[:, 12:16], looped[:, bass.ds(j, 1)], None, ALU.mult))
                            go(v.tensor_tensor(den, acc[:, ES:MS], sm[:, 8:12], ALU.mult))
                            go(v.tensor_tensor(den, den, sm[:, 12:16], ALU.add))
                            go(v.tensor_scalar(den, den, TINY, None, ALU.max))
                            go(v.reciprocal(den, den))
                            t.add(v.tensor_tensor(sm[:, 8:12], sm[:, 8:12], den, ALU.mult))
                            go(v.tensor_tensor(sm[:, 12:16], sm[:, 12:16], den, ALU.mult))
                            t.add(v.tensor_tensor(heads(acc[:, 0:D]), heads(acc[:, 0:D]), head_bcast(sm[:, 8:12]), ALU.mult))
                            go(v.tensor_tensor(heads(own[:, 0:D]), heads(own[:, 0:D]), head_bcast(sm[:, 12:16]), ALU.mult))
                            go(v.tensor_tensor(acc[:, 0:D], acc[:, 0:D], own[:, 0:D], ALU.add))
                            go(v.tensor_tensor(acc[:, 0:D], acc[:, 0:D], biases[:, n - 1, :], ALU.add))
                            v.tensor_scalar(tmp, acc[:, 0:D], 0.0, None, ALU.min).then_inc(s.neg, 1)
                            dve.wait_ge(s.negexp, j + 1)
                            go(v.scalar_tensor_tensor(acc[:, 0:D], acc[:, 0:D], 0.0, h, ALU.max, ALU.add))
                            if n == 1:
                                v.tensor_scalar(h, acc[:, 0:D], -1.0, None, ALU.add).then_inc(s.h, 1)
                            else:
                                go(v.scalar_tensor_tensor(xin, acc[:, 0:D], -1.0, xin, ALU.add, ALU.add))
                        if n != 1:
                            st = n_st[:, k, :]
                            go(v.bn_stats(st[:, 0:6], xin))
                            dve.sem_inc(s_passed, 1)
                            v.bn_aggr(st[:, 6:8], st[:, 0:6]).then_inc(s.var, 1)
                            dve.wait_ge(s.std, j + 1)
                            go(v.reciprocal(st[:, 9:10], st[:, 8:9]))
                            v.tensor_scalar(h, xin, st[:, 6:7], st[:, 9:10], ALU.subtract, ALU.mult).then_inc(s.h, 1)
                        o = n_out[:, k, :]
                        if n < 2:
                            if n == 1:
                                cnt, rest = sm[:, 28:36], sm[:, 36:44]
                                go(v.tensor_scalar(cnt, acc[:, RS:WIDE], 1.0, None, ALU.max))
                                go(v.reciprocal(cnt, cnt))
                                split(t, n_par[:, k, :].rearrange("p (r q) -> p r q", q=3), cnt, rest)
                            dve.wait_ge(s.mm, j + 1)
                            go(v.tensor_copy(o, bank[1][:, 0:TABLE]))
                            split(t, n_adp[:, k, :].rearrange("p (h q) -> p h q", q=3), o[:, D + HEADS:TABLE], sm[:, 44:48], s.res)
                        else:
                            go(v.tensor_tensor(xin, xin, biases[:, 2, :], ALU.add))
                            dve.wait_ge(s.mm, (j + 1) * 5)
                            v.tensor_tensor(o[:, 0:D], xin, bank[6][:, 0:D], ALU.add).then_inc(s.res, 1)
                        t.end()

            HT = [P, HEADS, TILES]

            def over_heads(ap):
                return ap.unsqueeze(1).to_broadcast(HT)

            def over_tiles(ap):
                return ap.unsqueeze(2).to_broadcast(HT)

            def edge_vec(n):
                s = es[n]
                per = (20, 19, 6)[n]
                w = width[n]
                with dve.Fori(0, turns) as i:
                    for u in range(2):
                        step = i * 2 + u
                        t = Turn(dve, s.vec, per, step)

                        def go(ins):
                            t.add(ins)
                            t.settle()

                        kf = keyf[:, u, :]
                        base = base_of[:, bass.ds(step + 1, 1)]
                        dve.wait_ge(s.loaded[u], (i + 1) * (16 * edge_loads_per_step[n]))
                        if n == 2:
                            v.scalar_tensor_tensor(row_i[:, u, :], src_i[:, u, :], float(N_REL), typ_i[:, u, :],
                                                   ALU.mult, ALU.add).then_inc(s.idx, 1)
                        go(v.tensor_scalar(kf, key_i[:, u, :], base, None, ALU.subtract))
                        v.tensor_tensor(onehot[:, u, :, :], kf[:, 1:TILES + 1].unsqueeze(2).to_broadcast([P, TILES, P]),
                                        iota_win[:].unsqueeze(1).to_broadcast([P, TILES, P]), ALU.is_equal).then_inc(s.hot, 1)
                        v.tensor_scalar(sel[:, u:u + 1], iota_part[:], base_of[:, bass.ds(step, 1)], base,
                                        ALU.add, ALU.is_equal).then_inc(s.sel, 1)
                        if n < 2:
                            df = differ[:, u, :]
                            go(v.tensor_tensor(df, kf[:, 1:KEYS], kf[:, 0:KEYS - 1], ALU.not_equal))
                            cu = cut[:, u, :]
                            t.add(v.tensor_scalar(by_head(cu[:, 0:HEADS * (TILES + 1)])[:, :, 1:TILES],
                                                  df[:, 1:TILES].unsqueeze(1).to_broadcast([P, HEADS, TILES - 1]), -BIG, None, ALU.mult))
                            t.add(v.tensor_scalar(edge_ends[:, u, 64:64 + HEADS], df[:, 0:1].to_broadcast([P, HEADS]), -BIG, None, ALU.mult))
                            t.add(v.tensor_scalar(edge_ends[:, u, 96:96 + HEADS], kf[:, TILES:TILES + 1].to_broadcast([P, HEADS]),
                                                  kf[:, 1:2], -BIG, ALU.not_equal, ALU.mult))
                            t.add(v.tensor_scalar(not_first[:, u, :], kf[:, 1:TILES + 1], kf[:, 1:2], -BIG, ALU.not_equal, ALU.mult))
                            t.add(v.tensor_scalar(not_final[:, u, :], kf[:, 1:TILES + 1], kf[:, TILES:TILES + 1], -BIG, ALU.not_equal, ALU.mult))
                            if n == 0:
                                t.add(v.tensor_tensor(rows[:, u, :, RS:WIDE], typ_i[:, u, :].unsqueeze(2).to_broadcast([P, TILES, N_REL]),
                                                      iota_rel[:].unsqueeze(1).to_broadcast([P, TILES, N_REL]), ALU.is_equal))
                            dve.wait_ge(s.dstv, step + 1)
                            go(v.tensor_reduce(z[:], bank[2][:, 0:TILES * 3 * HEADS].rearrange("p (t h q) -> p t h q", h=HEADS, q=3), AX.X, ALU.add))
                            dve.wait_ge(s.gathered[u], (i + 1) * (16 * TILES))
                            go(v.tensor_tensor(zz.rearrange("p h t -> p t h"), z[:], rows[:, u, :, D:D + HEADS], ALU.add))
                            scv = by_head(sc[:, :])[:, :, 0:TILES]
                            go(v.scalar_tensor_tensor(scv, zz[:], SLOPE, zz[:], ALU.mult, ALU.max))
                            L = HEADS * (TILES + 1)
                            go(v.tensor_tensor_scan(run_f[:], cu[:, 0:L], sc[:], -BIG, ALU.add, ALU.max))
                            go(v.tensor_tensor_scan(run_m[:, ::-1], cu[:, L:0:-1], run_f[:, ::-1], -BIG, ALU.add, ALU.max))
                            rm = by_head(run_m[:, :])[:, :, 0:TILES]
                            t.add(v.tensor_copy(edge_ends[:, u, 0:HEADS], rm[:, :, 0]))
                            t.settle()
                            v.tensor_copy(edge_ends[:, u, 32:32 + HEADS], rm[:, :, TILES - 1]).then_inc(s.ends, 1)
                            dve.wait_ge(s.seq, step + 1)
                            go(v.tensor_tensor_scan(seq_f[:, u, :], seq_c[:, 0:2 * P], seq_v[:], seq_f[:, 1 - u, 2 * P - 1:2 * P], ALU.add, ALU.max))
                            v.tensor_tensor_scan(seq_m[:, ::-1], seq_c[:, 2 * P:0:-1], seq_f[:, u, ::-1], -BIG, ALU.add, ALU.max).then_inc(s.seqm, 1)
                            dve.wait_ge(s.seqm, step + 1)
                            v.tensor_scalar(fac_d[:], seq_f[:, 1 - u, 2 * P - 1:2 * P], seq_m[:, 0:1], 0.0, ALU.subtract, ALU.min).then_inc(s.facd, 1)
                            dve.wait_ge(s.back, step + 1)
                            tm = by_head(tmp_m[:, :])[:, :, 0:TILES]
                            go(v.tensor_tensor(tm, over_tiles(bank[5][:, 0:HEADS]), over_heads(not_first[:, u, :]), ALU.add))
                            go(v.tensor_tensor(rm, rm, tm, ALU.max))
                            go(v.tensor_tensor(tm, over_tiles(bank[5][:, HEADS:2 * HEADS]), over_heads(not_final[:, u, :]), ALU.add))
                            go(v.tensor_tensor(rm, rm, tm, ALU.max))
                            v.tensor_tensor(zz[:], scv, rm, ALU.subtract).then_inc(s.expd, 1)
                            t.add(v.tensor_tensor(rows[:, u, :, MS:RS], by_head(run_m[:, :]).rearrange("p h t -> p t h")[:, 0:TILES, :],
                                                  df[:, 1:TILES + 1].unsqueeze(2).to_broadcast([P, TILES, HEADS]), ALU.mult))
                            dve.wait_ge(s.facr, step + 1)
                            v.tensor_tensor(carry[:, 0:w], fac_row[:, 0:w], bank[4][0:1, 0:w], ALU.mult).then_inc(s.carry, 1)
                            dve.wait_ge(s.exp, step + 1)
                            t.settle()
                            for t0, t1 in ((0, 7), (7, TILES)):
                                r = rows[:, u, t0:t1, 0:D].rearrange("p t (h d) -> p t h d", h=HEADS)
                                v.tensor_tensor(r, r, rows[:, u, t0:t1, ES:MS].unsqueeze(3).to_broadcast([P, t1 - t0, HEADS, HID]),
                                                ALU.mult).then_inc(s.rhs, 1)
                        else:
                            go(v.tensor_tensor(typ_hot[:], typ_i[:, u, :].unsqueeze(2).to_broadcast([P, TILES, N_REL]),
                                               iota_rel[:].unsqueeze(1).to_broadcast([P, TILES, N_REL]), ALU.is_equal))
                            dve.wait_ge(s.dstv, step + 1)
                            go(v.tensor_reduce(ic[:], bank[2][:, 0:TILES * 3 * N_REL].rearrange("p (t r q) -> p t r q", r=N_REL, q=3), AX.X, ALU.add))
                            go(v.tensor_tensor(ic[:], ic[:], typ_hot[:], ALU.mult))
                            go(v.tensor_reduce(coef[:], ic[:], AX.X, ALU.add))
                            go(v.tensor_tensor(coef[:], coef[:], wts[:, u, :], ALU.mult))
                            dve.wait_ge(s.pick, step + 1)
                            v.tensor_copy(carry[0:1, 0:D], bank[4][0:1, 0:D]).then_inc(s.carry, 1)
                            dve.wait_ge(s.gathered[u], (i + 1) * (16 * TILES))
                            for t0, t1 in ((0, 7), (7, TILES)):
                                r = rows[:, u, t0:t1, 0:D]
                                v.tensor_tensor(r, r, coef[:, t0:t1].unsqueeze(2).to_broadcast([P, t1 - t0, D]), ALU.mult).then_inc(s.rhs, 1)
                            dve.wait_ge(s.acc, step + 2)
                            v.tensor_tensor(out_sb[:, u, :], bank[6 + u][:, 0:D], win_root[:, u, :], ALU.add).then_inc(s.outw, 1)
                        t.end()

            for n in range(3):
                node_vec(n)
                edge_vec(n)


def kernel(**inputs):
    import numpy as _np
    import concourse.bacc as _bacc
    from concourse import mybir as _mybir
    from concourse.bass_utils import run_bass_kernel_spmd as _run

    a = {k: _np.ascontiguousarray(v) for k, v in inputs.items()}
    pad = (N_CHUNKS + 1) * CHUNK - N_EDGES

    def padded(v, value):
        return _np.concatenate([v, _np.full(pad, value, v.dtype)])

    def in_partitions(v):
        return v.reshape(-1, TILES)

    keys = padded(a["dst"], PAD_KEY)
    before = _np.concatenate([_np.full(1, -1, keys.dtype), keys])[:-1]
    after = _np.concatenate([keys, _np.full(1, PAD_KEY, keys.dtype)])[1:]
    host = {
        "x": _np.concatenate([a["x"], _np.zeros((NP - N_NODES, D), a["x"].dtype)]),
        "edge_records": _np.concatenate([
            in_partitions(before)[:, :1], in_partitions(keys), in_partitions(after)[:, -1:],
            in_partitions(padded(a["src"], 0)), in_partitions(padded(a["edge_type_8"], 0))], axis=1),
        "chunk_firsts": keys[None, 0:N_CHUNKS * CHUNK:CHUNK],
        "chunk_lasts": keys[None, CHUNK - 1:N_CHUNKS * CHUNK:CHUNK],
        "edge_weight": in_partitions(padded(a["edge_weight"], 0)),
    }
    for k in ("W1", "att_src1", "att_dst1", "b1", "W2", "att_src2", "att_dst2", "b2"):
        host[k] = a["L0_gnn_" + k]
    for k in ("weight", "root", "bias"):
        host[k] = a["L1_gnn_" + k]

    nc = _bacc.Bacc("TRN2", target_bir_lowering=False, num_devices=1)
    arrays, args = {}, []
    for name, v in host.items():
        arrays[f"in_{name}"] = v = _np.ascontiguousarray(v)
        args.append(nc.dram_tensor(f"in_{name}", v.shape, _mybir.dt.from_np(v.dtype), kind="ExternalInput").ap())
    args.append(nc.dram_tensor("out_0", (NP, D), _mybir.dt.float32, kind="ExternalOutput").ap())
    build(nc, *args)
    r = _run(nc, [arrays], core_ids=[0])
    return r.results[0]["out_0"][:N_NODES]
```

```python
import concourse.bass as bass
from concourse import mybir
from contextlib import ExitStack

F32 = mybir.dt.float32
BF16 = mybir.dt.bfloat16
I32 = mybir.dt.int32
ALU = mybir.AluOpType
ACT = mybir.ActivationFunctionType
AX = mybir.AxisListType

P = 128
N_NODES = 12500
N_EDGES = 212500
N_LOOPED = 6250
D = 256
HEADS = 4
HID = 64
N_REL = 8
SLOPE = 0.2
EPS = 1e-5
BIG = 1e30
TINY = 1e-30

TILES = 13
CHUNK = TILES * P
N_CHUNKS = -(-N_EDGES // CHUNK)
GROUP = 3
HALVES = 2
NODE_TURNS = -(-(N_NODES + P) // (P * GROUP * HALVES))
NODE_TILES = NODE_TURNS * HALVES * GROUP
NP = NODE_TILES * P
TAIL = N_NODES // P
RING = 4
DVE_PARTS = ((0, 4), (4, 8), (8, TILES - 1))
ACT_TILE = TILES - 1
MAX_TURNS = -(-(N_CHUNKS + N_NODES // P) // RING)
MAX_STEPS = (MAX_TURNS + 2) * RING
PAD_KEY = 1 << 20
KEYS = TILES + 2
RECORD = KEYS + 2 * TILES

TABLE = D + 2 * HEADS
ES, MS, RS = D, D + HEADS, D + 2 * HEADS
WIDE = TABLE + N_REL


class Turn:

    def __init__(self, engine, sem, per_turn, turn):
        self.engine, self.sem, self.per_turn, self.turn, self.count = engine, sem, per_turn, turn, 0

    def add(self, instruction):
        instruction.then_inc(self.sem, 1)
        self.count += 1

    def settle(self):
        self.engine.wait_ge(self.sem, self.turn * self.per_turn + self.count)

    def end(self):
        assert self.count == self.per_turn, (self.count, self.per_turn)


def build(nc, x, records, firsts, lasts, ewt, W1, as1, ad1, b1, W2, as2, ad2, b2, Wr, root, rbias, out):
    assert N_CHUNKS == P

    def dram(name, shape, dt):
        return nc.dram_tensor(name, shape, dt, kind="Internal").ap()

    tables = [dram("node_rows_1", (NP, TABLE), F32), dram("node_rows_2", (NP, TABLE), F32)]
    ads = [dram("a_dst_parts_1", (NP, 3 * HEADS), BF16), dram("a_dst_parts_2", (NP, 3 * HEADS), BF16)]
    accs = [dram("edge_sums_1", (NP, WIDE), F32), dram("edge_sums_2", (NP, WIDE), F32)]
    icd = dram("inverse_count_parts", (NP, 3 * N_REL), BF16)
    yrel = dram("relation_rows", (NP, N_REL * D), F32)
    rootd = dram("root_rows", (NP, D), F32)
    yrows = yrel.rearrange("n (r d) -> (n r) d", r=N_REL)

    ctx = ExitStack()
    with ctx:
        def sb(name, shape, dt=F32):
            return ctx.enter_context(nc.sbuf_tensor(name, shape, dt))

        def sem(name):
            return ctx.enter_context(nc.semaphore(name))

        psum = ctx.enter_context(nc.psum_tensor("psum", [P, 8, 512], F32))
        bank = [psum[:, i, :] for i in range(8)]

        ident = sb("ident", [P, P])
        identb = sb("identb", [P, P], BF16)
        ones = sb("ones", [P, P])
        iota_win = sb("iota_win", [P, P])
        iota_part = sb("iota_part", [P, 1])
        iota_steps = sb("iota_steps", [P, MAX_STEPS])
        iota_rel = sb("iota_rel", [P, N_REL])
        eps_t = sb("eps_t", [P, 1])
        minus_one = sb("minus_one", [P, 1])
        head_rows = sb("head_rows", [HEADS + 1, WIDE])
        first_row = sb("first_row", [1, P])
        node_no = sb("node_no", [P, NODE_TILES])
        looped = sb("looped", [P, NODE_TILES])
        loop_bias = sb("loop_bias", [P, NODE_TILES])

        ends_i = sb("ends_i", [1, 2, P], I32)
        ends = sb("ends", [1, 2, P])
        plan = sb("plan", [1, 6, P])
        plan_i = sb("plan_i", [1, P], I32)
        cols = sb("cols", [P, 3])
        hot = sb("hot", [P, 4, MAX_STEPS])
        base_of = sb("base_of", [P, MAX_STEPS + 1])
        step_i = sb("step_i", [1, 2, MAX_STEPS], I32)
        prev_i = sb("prev_i", [1, MAX_STEPS], I32)
        turns_i = sb("turns_i", [1, 2], I32)

        wx = [sb("w1x", [P, 2, TABLE]), sb("w2x", [P, 2, TABLE])]
        att = sb("att", [P, 4, D])
        att_tmp = sb("att_tmp", [P, 2, D])
        biases = sb("biases", [P, 3, D])
        wrel = sb("wrel", [P, 2, N_REL + 1, D])

        shared = sb("shared", [P, RING * TILES * WIDE])
        rows = shared[:, :].rearrange("p (u t w) -> p u t w", u=RING, t=TILES)
        taken = [0]

        def shared_buffer(*shape):
            n = 1
            for q in shape:
                n *= q
            taken[0] += n
            assert taken[0] <= RING * TILES * WIDE
            flat = shared[:, taken[0] - n:taken[0]]
            if len(shape) == 2:
                return flat.rearrange("p (b d) -> p b d", b=shape[0])
            return flat.rearrange("p (b k d) -> p b k d", b=shape[0], k=shape[1])

        KN = HALVES
        n_x = shared_buffer(KN, GROUP, D)
        n_own = shared_buffer(KN, GROUP, TABLE)
        n_acc = shared_buffer(KN, GROUP, WIDE)
        n_st = sb("n_st", [P, KN, GROUP, 10])
        n_h = shared_buffer(KN, GROUP, D)
        n_neg = shared_buffer(KN, GROUP, D)
        n_hT = sb("n_hT", [P, 2, 2, P])
        n_out = shared_buffer(KN, GROUP, TABLE)
        n_y = shared_buffer(2, N_REL * D)
        n_par = sb("n_par", [P, KN, GROUP, 3 * N_REL], BF16)
        n_adp = sb("n_adp", [P, KN, GROUP, 3 * HEADS], BF16)
        n_sm = sb("n_sm", [P, KN, 12, GROUP, HEADS])
        n_cnt = sb("n_cnt", [P, KN, 2, GROUP, N_REL])

        record = sb("record", [P, RING, RECORD], I32)
        key_i = record[:, :, 0:KEYS]
        src_i = record[:, :, KEYS:KEYS + TILES]
        typ_i = record[:, :, KEYS + TILES:RECORD]
        row_i = sb("row_i", [P, RING, TILES], I32)
        wts = sb("wts", [P, RING, TILES])
        keyf = sb("keyf", [P, RING, KEYS])
        win_ad = sb("win_ad", [P, RING, 3 * HEADS], BF16)
        win_ic = sb("win_ic", [P, RING, 3 * N_REL], BF16)
        win_root = sb("win_root", [P, RING, D])
        onehot = sb("onehot", [P, RING, TILES, P])
        onehot_b = sb("onehot_b", [P, TILES, P], BF16)
        onehot_T = sb("onehot_T", [P, TILES, P], BF16)
        differ = sb("differ", [P, 2, TILES + 1])
        cut = sb("cut", [P, 2, HEADS * (TILES + 1) + 1])
        sc = sb("sc", [P, HEADS * (TILES + 1)])
        run_f = sb("run_f", [P, HEADS * (TILES + 1)])
        run_m = sb("run_m", [P, HEADS * (TILES + 1)])
        tmp_m = sb("tmp_m", [P, HEADS * (TILES + 1)])
        tmp_n = sb("tmp_n", [P, HEADS, TILES])
        z = sb("z", [P, TILES, HEADS])
        zz = sb("zz", [P, HEADS, TILES])
        not_first = sb("not_first", [P, 2, TILES])
        not_final = sb("not_final", [P, 2, TILES])
        edge_ends = sb("edge_ends", [P, 2, P])
        seq_v = sb("seq_v", [HEADS, 2 * P])
        seq_c = sb("seq_c", [HEADS, 2 * P + 1])
        seq_f = sb("seq_f", [HEADS, 2, 2 * P])
        seq_m = sb("seq_m", [HEADS, 2 * P])
        fac_d = sb("fac_d", [HEADS, 1])
        fac = sb("fac", [HEADS + 1, 1])
        fac_row = sb("fac_row", [1, WIDE])
        carry = sb("carry", [1, WIDE])
        sel = sb("sel", [P, 2])
        acc_sb = sb("acc_sb", [P, 2, WIDE])
        out_sb = sb("out_sb", [P, 2, D])
        typ_hot = sb("typ_hot", [P, TILES, N_REL])
        ic = sb("ic", [P, TILES, N_REL])
        coef = sb("coef", [P, 2, TILES])
        zeros_t = sb("zeros_t", [P, WIDE])

        s_const = sem("s_const")
        s_wload = sem("s_wload")
        s_vplan = sem("s_vplan")
        s_plan_row = sem("s_plan_row")
        s_plan_col = sem("s_plan_col")
        s_plan_hot = sem("s_plan_hot")
        s_plan_sum = sem("s_plan_sum")
        s_plan = sem("s_plan")
        s_zeroed = sem("s_zeroed")
        s_cleared = sem("s_cleared")
        s_pool = sem("s_pool")
        s_passed = sem("s_passed")

        class NodeSems:

            def __init__(self, n):
                self.loaded = [sem(f"n{n}_loaded{b}") for b in range(HALVES)]
                self.stored = [sem(f"n{n}_stored{b}") for b in range(HALVES)]
                self.vec = sem(f"n{n}_vec")
                if n > 0:
                    self.dist = sem(f"n{n}_dist")
                    self.wexp = sem(f"n{n}_wexp")
                    self.conv = sem(f"n{n}_conv")
                    self.neg = sem(f"n{n}_neg")
                    self.negexp = sem(f"n{n}_negexp")
                if n != 1:
                    self.var = sem(f"n{n}_var")
                    self.std = sem(f"n{n}_std")
                self.h = sem(f"n{n}_h")
                self.hT = sem(f"n{n}_hT")
                self.hTs = sem(f"n{n}_hTs")
                self.mm = sem(f"n{n}_mm")
                self.res = sem(f"n{n}_res")
                if n < 2:
                    self.prod = sem(f"n{n}_prod")
                else:
                    self.copied = sem("n2_copied")
                    self.ystored = [sem(f"n2_ystored{y}") for y in range(2)]
                    self.rootr = sem("n2_rootr")

        class EdgeSems:

            def __init__(self, n):
                self.loaded = [sem(f"e{n}_loaded{u}") for u in range(RING)]
                self.gathered = [sem(f"e{n}_gathered{u}") for u in range(RING)]
                self.stored = sem(f"e{n}_stored")
                self.prep = sem(f"e{n}_prep")
                self.vec = sem(f"e{n}_vec")
                self.hot = sem(f"e{n}_hot")
                self.hotb = sem(f"e{n}_hotb")
                self.hotT = sem(f"e{n}_hotT")
                self.hotTs = sem(f"e{n}_hotTs")
                self.dstv = sem(f"e{n}_dstv")
                self.sel = sem(f"e{n}_sel")
                self.pick = sem(f"e{n}_pick")
                self.carry = sem(f"e{n}_carry")
                self.read = sem(f"e{n}_read")
                self.rhs = sem(f"e{n}_rhs")
                self.share = sem(f"e{n}_share")
                self.done = sem(f"e{n}_done")
                self.acc = sem(f"e{n}_acc")
                if n < 2:
                    self.ends = sem(f"e{n}_ends")
                    self.endsT = sem(f"e{n}_endsT")
                    self.seq = sem(f"e{n}_seq")
                    self.seqm = sem(f"e{n}_seqm")
                    self.back = sem(f"e{n}_back")
                    self.facd = sem(f"e{n}_facd")
                    self.fac = sem(f"e{n}_fac")
                    self.facr = sem(f"e{n}_facr")
                    self.expd = sem(f"e{n}_expd")
                    self.exp = sem(f"e{n}_exp")
                else:
                    self.coef = sem(f"e{n}_coef")
                    self.idx = sem(f"e{n}_idx")
                    self.outw = sem(f"e{n}_outw")

        ns = [NodeSems(n) for n in range(3)]
        es = [EdgeSems(n) for n in range(3)]

        block = ctx.enter_context(nc.Block())

        def by_head(t, n=TILES + 1, part=P):
            return t.rearrange("p (h t) -> p h t", h=HEADS)

        x_v = x.rearrange("(j p) d -> j p d", p=P)

        n_stores = (2, 3, 1)
        edge_loads_per_step = (2, 2, 4)
        width = (WIDE, TABLE, D)

        def group_rows(ap, g):
            return ap[bass.ds(g * (GROUP * P), GROUP * P), :].rearrange("(k p) d -> p k d", p=P)

        def tile_rows(ap, j):
            return ap[bass.ds(j * P, P), :]

        @block.sync
        def _(sp):
            sp.dma_start(ends_i[0:1, 0, :], firsts).then_inc(s_wload, 16)
            sp.dma_start(ends_i[0:1, 1, :], lasts).then_inc(s_wload, 16)
            for t, W in ((wx[0], W1), (wx[1], W2)):
                sp.dma_start(t[:, :, 0:D], W.rearrange("(k p) n -> p k n", p=P)).then_inc(s_wload, 16)
            for q, a in enumerate((as1, ad1, as2, ad2)):
                sp.dma_start(att[:, q, :], a.rearrange("h d -> (h d)").partition_broadcast(P)).then_inc(s_wload, 16)
            for q, b in enumerate((b1, b2, rbias)):
                sp.dma_start(biases[:, q, :], b.partition_broadcast(P)).then_inc(s_wload, 16)
            for r in range(N_REL):
                sp.dma_start(wrel[:, :, r, :], Wr[r].rearrange("(k p) n -> p k n", p=P)).then_inc(s_wload, 16)
            sp.dma_start(wrel[:, :, N_REL, :], root.rearrange("(k p) n -> p k n", p=P)).then_inc(s_wload, 16)
            sp.wait_ge(s_const, 1)
            for a in accs:
                for j in range(TAIL, NODE_TILES):
                    sp.dma_start(a[j * P:(j + 1) * P, :], zeros_t[:, :]).then_inc(s_zeroed, 16)
            sp.wait_ge(s_zeroed, 2 * 16 * (NODE_TILES - TAIL))
            sp.wait_ge(s_plan, 1)
            turns = nc.sync.value_load(turns_i[0:1, 1:2], min_val=1, max_val=MAX_TURNS)

            def node_loads(n):
                s = ns[n]
                with sp.Fori(0, NODE_TURNS) as i:
                    for b in range(HALVES):
                        sp.wait_ge(s.stored[b], i * (16 * n_stores[n]) + 16)
                        g = i * HALVES + b
                        if n != 1:
                            sp.dma_start(n_x[:, b, :, :], group_rows(x, g)).then_inc(s.loaded[b], 16)
                        if n > 0:
                            sp.dma_start(n_acc[:, b, :, 0:width[n - 1]],
                                         group_rows(accs[n - 1], g)[:, :, 0:width[n - 1]]).then_inc(s.loaded[b], 16)
                            sp.dma_start(n_own[:, b, :, :], group_rows(tables[n - 1], g)).then_inc(s.loaded[b], 16)

            def edge_loads(n):
                s = es[n]

                def load(step, u):
                    r0 = nc.sync.value_load(step_i[0:1, 0, bass.ds(step, 1)], min_val=0, max_val=N_CHUNKS * P)
                    b0 = nc.sync.value_load(step_i[0:1, 1, bass.ds(step, 1)], min_val=0, max_val=N_NODES)
                    if n < 2:
                        sp.wait_ge(s.done, step + 1)
                    else:
                        sp.wait_ge(s.outw, step + 2)
                    sp.dma_start(record[:, u, :], records[bass.ds(r0, P), :]).then_inc(s.loaded[u], 16)
                    if n < 2:
                        sp.dma_start(win_ad[:, u, :], ads[n][bass.ds(b0, P), :]).then_inc(s.loaded[u], 16)
                    else:
                        sp.dma_start(wts[:, u, :], ewt[bass.ds(r0, P), :]).then_inc(s.loaded[u], 16)
                        sp.dma_start(win_ic[:, u, :], icd[bass.ds(b0, P), :]).then_inc(s.loaded[u], 16)
                        sp.dma_start(win_root[:, u, :], rootd[bass.ds(b0, P), :]).then_inc(s.loaded[u], 16)

                load(0, 0)
                load(1, 1)
                with sp.Fori(0, turns) as i:
                    for u in range(RING):
                        load(i * RING + (u + 2), (u + 2) % RING)

            for n in range(3):
                node_loads(n)
                for b in range(HALVES):
                    sp.wait_ge(ns[n].stored[b], 16 + NODE_TURNS * 16 * n_stores[n])
                if n == 2:
                    for y in range(2):
                        sp.wait_ge(ns[n].ystored[y], 16 + NODE_TILES // 2 * 16)
                edge_loads(n)
                sp.wait_ge(es[n].stored, turns * (16 * RING) + (16 if n < 2 else 32))
                sp.sem_inc(s_passed, 1)


        @block.gpsimd
        def _(pool):
            g = nc.gpsimd
            g.memset(ident[:], 0.0)
            g.memset(identb[:], 0.0)
            g.memset(ones[:], 1.0)
            g.memset(eps_t[:], EPS)
            g.memset(minus_one[:], -1.0)
            g.memset(win_root[:], 0.0)
            g.memset(zeros_t[:], 0.0)
            g.memset(acc_sb[:], 0.0)
            g.memset(edge_ends[:], 0.0)
            g.memset(cut[:], -BIG)
            g.memset(sc[:], -BIG)
            g.memset(seq_c[:], 0.0)
            g.memset(seq_f[:], -BIG)
            g.memset(fac[:], 1.0)
            g.memset(first_row[:], 0.0)
            g.memset(base_of[:], -4.0 * PAD_KEY)
            g.memset(head_rows[:], 0.0)
            g.iota(iota_win[:], [[1, P]], base=0, channel_multiplier=0, allow_small_or_imprecise_dtypes=True)
            g.iota(iota_part[:], [[0, 1]], base=0, channel_multiplier=1, allow_small_or_imprecise_dtypes=True)
            g.iota(iota_steps[:], [[1, MAX_STEPS]], base=0, channel_multiplier=0, allow_small_or_imprecise_dtypes=True)
            g.iota(iota_rel[:], [[1, N_REL]], base=0, channel_multiplier=0, allow_small_or_imprecise_dtypes=True)
            g.iota(node_no[:], [[P, NODE_TILES]], base=0, channel_multiplier=1,
                   allow_small_or_imprecise_dtypes=True).then_inc(s_pool, 1)
            pool.wait_ge(s_pool, 1)
            g.memset(first_row[0:1, 0:1], 1.0)
            g.affine_select(out=ident[:], in_=ident[:], compare_op=ALU.not_equal, fill=1.0, base=0,
                            pattern=[[-1, P]], channel_multiplier=1)
            g.affine_select(out=identb[:], in_=identb[:], compare_op=ALU.not_equal, fill=1.0, base=0,
                            pattern=[[-1, P]], channel_multiplier=1)
            g.affine_select(out=head_rows[:, 0:D], in_=head_rows[:, 0:D], compare_op=ALU.not_equal, fill=1.0, base=0,
                            pattern=[[-1, HEADS], [0, HID]], channel_multiplier=1)
            g.affine_select(out=head_rows[:, ES:MS], in_=head_rows[:, ES:MS], compare_op=ALU.not_equal, fill=1.0,
                            base=0, pattern=[[-1, HEADS]], channel_multiplier=1)
            g.affine_select(out=head_rows[:, RS:WIDE], in_=head_rows[:, RS:WIDE], compare_op=ALU.not_equal, fill=1.0,
                            base=-HEADS, pattern=[[0, N_REL]], channel_multiplier=1)
            g.tensor_scalar(looped[:], node_no[:], float(N_LOOPED), None, ALU.is_lt).then_inc(s_pool, 1)
            pool.wait_ge(s_pool, 2)
            g.tensor_scalar(loop_bias[:], looped[:], -1.0, BIG, ALU.add, ALU.mult).then_inc(s_const, 1)

            pool.wait_ge(s_plan, 1)
            turns = g.value_load(turns_i[0:1, 1:2], min_val=1, max_val=MAX_TURNS)

            def gathers(n):
                s = es[n]
                with pool.Fori(0, turns) as i:
                    for u in range(RING):
                        if n < 2:
                            pool.wait_ge(s.loaded[u], (i + 1) * (16 * edge_loads_per_step[n]))
                        else:
                            pool.wait_ge(s.idx, i * RING + (u + 1))
                        pool.sem_inc(s_passed, 1)
                        for t in range(TILES):
                            if n < 2:
                                g.indirect_dma_start(
                                    out=rows[:, u, t, 0:TABLE], out_offset=None, in_=tables[n][:, :],
                                    in_offset=bass.IndirectOffsetOnAxis(ap=src_i[:, u, t:t + 1], axis=0),
                                ).then_inc(s.gathered[u], 16)
                            else:
                                g.indirect_dma_start(
                                    out=rows[:, u, t, 0:D], out_offset=None, in_=yrows[:, :],
                                    in_offset=bass.IndirectOffsetOnAxis(ap=row_i[:, u, t:t + 1], axis=0),
                                ).then_inc(s.gathered[u], 16)

            for n in range(3):
                gathers(n)

        @block.scalar
        def _(act):
            a = nc.scalar
            for n in range(3):
                for b in range(HALVES):
                    act.sem_inc(ns[n].stored[b], 16)
            for y in range(2):
                act.sem_inc(ns[2].ystored[y], 16)
            act.wait_ge(s_plan, 1)
            turns = a.value_load(turns_i[0:1, 1:2], min_val=1, max_val=MAX_TURNS)

            def node_act(n):
                s = ns[n]

                def weights(g, b):
                    act.wait_ge(s.dist, g + 1)
                    a.activation(n_sm[:, b, 2:4, :, :], n_sm[:, b, 0:2, :, :], ACT.Exp).then_inc(s.wexp, 1)

                def elu(g, b):
                    act.wait_ge(s.conv, g + 1)
                    a.activation(n_neg[:, b, :, :], n_acc[:, b, :, 0:D], ACT.Relu, scale=-1.0).then_inc(s.neg, 1)
                    act.wait_ge(s.neg, g + 1)
                    a.activation(n_h[:, b, :, :], n_neg[:, b, :, :], ACT.Exp, scale=-1.0).then_inc(s.negexp, 1)

                def deviation(g, b):
                    act.wait_ge(s.var, g + 1)
                    a.activation(n_st[:, b, :, 8:9], n_st[:, b, :, 7:8], ACT.Sqrt, bias=eps_t[:, 0:1]).then_inc(s.std, 1)

                def transposed(g, k, y):
                    j = g * GROUP + k
                    act.wait_ge(s.hT, j + 1)
                    src_ = bank[y][:, 0:D].rearrange("p (c q) -> p c q", c=2)
                    if n == 1:
                        a.activation(n_hT[:, y, :, :], src_, ACT.Identity, bias=minus_one[:, 0:1]).then_inc(s.hTs, 1)
                    else:
                        a.activation(n_hT[:, y, :, :], src_, ACT.Relu).then_inc(s.hTs, 1)

                with act.Fori(0, NODE_TURNS) as i:
                    first, second = i * HALVES, i * HALVES + 1
                    if n > 0:
                        weights(first, 0)
                        elu(first, 0)
                        weights(second, 1)
                        if n == 2:
                            deviation(first, 0)
                        elu(second, 1)
                        if n == 2:
                            deviation(second, 1)
                    else:
                        deviation(first, 0)
                        deviation(second, 1)
                    for b, g in ((0, first), (1, second)):
                        for k in range(GROUP):
                            y = (b * GROUP + k) % 2
                            if n < 2:
                                transposed(g, k, y)
                            else:
                                j = g * GROUP + k
                                transposed(g, k, y)
                                act.wait_ge(s.ystored[y], (i * GROUP + (b * GROUP + k) // 2) * 16 + 16)
                                for q in range(4):
                                    act.wait_ge(s.mm, j * 5 + (q + 1))
                                    a.activation(n_y[:, y, q * 512:(q + 1) * 512], bank[2 + q][:, :], ACT.Copy).then_inc(s.copied, 1)
                                act.wait_ge(s.copied, (j + 2) * 4)
                                act.dma_start(tile_rows(yrel, j), n_y[:, y, :]).then_inc(s.ystored[y], 16)
                        if n < 2:
                            act.wait_ge(s.mm, (g + 1) * GROUP)
                            a.activation(n_out[:, b, :, :], psum[:, 2:2 + GROUP, 0:TABLE], ACT.Copy).then_inc(s.prod, 1)
                    for b, g in ((0, first), (1, second)):
                        act.wait_ge(s.res, g + 2)
                        if n < 2:
                            act.dma_start(group_rows(tables[n], g), n_out[:, b, :, :]).then_inc(s.stored[b], 16)
                            act.dma_start(group_rows(ads[n], g), n_adp[:, b, :, :]).then_inc(s.stored[b], 16)
                            if n == 1:
                                act.dma_start(group_rows(icd, g), n_par[:, b, :, :]).then_inc(s.stored[b], 16)
                        else:
                            act.dma_start(group_rows(rootd, g), n_out[:, b, :, 0:D]).then_inc(s.stored[b], 16)

            def edge_act(n):
                s = es[n]
                w = width[n]

                def hot_bf16(step, u):
                    act.wait_ge(s.hot, step + 1)
                    a.activation(onehot_b[:], onehot[:, u, :, :], ACT.Copy).then_inc(s.hotb, 1)

                def hot_transposed(step):
                    act.wait_ge(s.hotT, step + 1)
                    for half, (t0, t1) in enumerate(((0, 7), (7, TILES))):
                        last = a.activation(
                            onehot_T[:, t0:t1, :],
                            bank[half].bitcast(BF16)[:, 0:(t1 - t0) * P].rearrange("p (t m) -> p t m", m=P), ACT.Copy)
                    last.then_inc(s.hotTs, 1)

                def store_out(step, slot):
                    b0 = a.value_load(prev_i[0:1, bass.ds(step, 1)], min_val=0, max_val=N_NODES)
                    act.wait_ge(s.stored, step * 16 + 16)
                    act.wait_ge(s.outw, step + (RING + 1))
                    act.dma_start(out[bass.ds(b0, P), :], out_sb[:, slot, :]).then_inc(s.stored, 16)

                hot_bf16(0, 0)
                hot_transposed(0)
                with act.Fori(0, turns) as i:
                    for u in range(RING):
                        step = i * RING + u
                        if n < 2:
                            act.wait_ge(s.endsT, step + 1)
                            a.activation(seq_v[:, 0::2], bank[3][0:HEADS, 0:P], ACT.Copy)
                            a.activation(seq_v[:, 1::2], bank[3][32:32 + HEADS, 0:P], ACT.Copy)
                            a.activation(seq_c[:, 0:2 * P:2], bank[3][64:64 + HEADS, 0:P], ACT.Copy)
                            a.activation(seq_c[:, 1:2 * P:2], bank[3][96:96 + HEADS, 0:P], ACT.Copy).then_inc(s.seq, 1)
                            hot_bf16(step + 1, (u + 1) % RING)
                            act.wait_ge(s.facd, step + 1)
                            a.activation(fac[0:HEADS, :], fac_d[:, :], ACT.Exp).then_inc(s.fac, 1)
                            act.wait_ge(s.expd, step + 1)
                            a.activation(rows[:, u, :, ES:MS], zz.rearrange("p h t -> p t h"), ACT.Exp).then_inc(s.exp, 1)
                            act.wait_ge(s.pick, step + 1)
                            a.activation(fac_row[:, 0:w], bank[3][0:1, 0:w], ACT.Copy).then_inc(s.facr, 1)
                            hot_transposed(step + 1)
                            act.wait_ge(s.exp, step + 1)
                            for h in range(HEADS):
                                r = rows[:, u, ACT_TILE, h * HID:(h + 1) * HID]
                                last = a.activation(r, r, ACT.Copy, scale=rows[:, u, ACT_TILE, ES + h:ES + h + 1])
                            last.then_inc(s.share, 1)
                        else:
                            hot_bf16(step + 1, (u + 1) % RING)
                            act.wait_ge(s.coef, step + 1)
                            act.wait_ge(s.gathered[u], (i + 1) * (16 * TILES))
                            r = rows[:, u, ACT_TILE, 0:D]
                            a.activation(r, r, ACT.Copy, scale=coef[:, u % 2, ACT_TILE:ACT_TILE + 1]).then_inc(s.share, 1)
                            hot_transposed(step + 1)
                        if n == 2:
                            store_out(step, 1 - u % 2)
                        act.wait_ge(s.done, step + (RING + 1))
                        a.activation(acc_sb[:, u % 2, 0:w], bank[6 + u % 2][:, 0:w], ACT.Copy).then_inc(s.acc, 1)
                        if n < 2:
                            b0 = a.value_load(step_i[0:1, 1, bass.ds(step, 1)], min_val=0, max_val=N_NODES)
                            act.wait_ge(s.stored, step * 16 + 16)
                            act.wait_ge(s.acc, step + 2)
                            act.dma_start(accs[n][bass.ds(b0, P), 0:w], acc_sb[:, u % 2, 0:w]).then_inc(s.stored, 16)
                if n == 2:
                    store_out(turns * RING, 1)

            for n in range(3):
                node_act(n)
                act.sem_inc(es[n].stored, 16)
                edge_act(n)

        @block.tensor
        def _(pe):
            t_ = nc.tensor
            for n in range(3):
                pe.sem_inc(es[n].done, RING)
            pe.wait_ge(s_const, 1)
            pe.wait_ge(s_plan_row, 1)
            for q, row in enumerate((3, 4, 5)):
                last = t_.matmul(bank[0][:, q:q + 1], plan[0:1, row, :], ones[0:1, 0:1], start=True, stop=True)
            last.then_inc(s_plan_col, 1)
            pe.wait_ge(s_plan_hot, 1)
            for q, m in enumerate((0, 2, 3)):
                last = t_.matmul(bank[1 + q][:, 0:MAX_STEPS], ones[:, :], hot[:, m, :], start=True, stop=True)
            last.then_inc(s_plan_sum, 1)
            pe.wait_ge(s_plan, 1)
            turns = t_.value_load(turns_i[0:1, 1:2], min_val=1, max_val=MAX_TURNS)

            def node_pe(n):
                s = ns[n]

                def transpose(g, b, k, y):
                    pe.wait_ge(s.hTs, g * GROUP + (k + 1))
                    for c in range(2):
                        last = t_.transpose(bank[y][:, c * P:(c + 1) * P], n_h[:, b, k, c * P:(c + 1) * P], ident[:])
                    last.then_inc(s.hT, 1)

                with pe.Fori(0, NODE_TURNS) as i:
                    for b in range(HALVES):
                        g = i * HALVES + b
                        pe.wait_ge(s.h, g + 1)
                        if n < 2:
                            pe.wait_ge(s.prod, g + 1)
                        for k in range(GROUP):
                            y = (b * GROUP + k) % 2
                            j = g * GROUP + k
                            if k == 0:
                                transpose(g, b, 0, y)
                            if k + 1 < GROUP:
                                transpose(g, b, k + 1, 1 - y)
                            pe.wait_ge(s.hTs, j + 3)
                            if n < 2:
                                for c in range(2):
                                    last = t_.matmul(bank[2 + k][:, 0:TABLE], n_hT[:, y, c, :], wx[n][:, c, :], start=(c == 0), stop=(c == 1))
                                last.then_inc(s.mm, 1)
                            else:
                                for q in range(5):
                                    if q < 4:
                                        pe.wait_ge(s.copied, j * 4 + (q + 1))
                                    else:
                                        pe.wait_ge(s.rootr, j + 1)
                                    w = 2 if q < 4 else 1
                                    for c in range(2):
                                        last = t_.matmul(bank[2 + q][:, 0:w * D], n_hT[:, y, c, :],
                                                         wrel[:, c, 2 * q:2 * q + w, :], start=(c == 0), stop=(c == 1))
                                    last.then_inc(s.mm, 1)

            def edge_pe(n):
                s = es[n]
                w = width[n]

                def transpose_hot(step):
                    pe.wait_ge(s.hotb, step + 1)
                    for t in range(TILES):
                        b, o = (0, t) if t < 7 else (1, t - 7)
                        last = t_.transpose(bank[b].bitcast(BF16)[:, o * P:(o + 1) * P], onehot_b[:, t, :], identb[:])
                    last.then_inc(s.hotT, 1)

                def look_up(step, u):
                    pe.wait_ge(s.hotTs, step + 1)
                    pe.wait_ge(s.read, step + 1)
                    nv = 3 * HEADS if n < 2 else 3 * N_REL
                    win = win_ad if n < 2 else win_ic
                    for t in range(TILES):
                        last = t_.matmul(bank[2][:, t * nv:(t + 1) * nv], onehot_T[:, t, :], win[:, u, :], start=True, stop=True)
                    last.then_inc(s.dstv, 1)

                transpose_hot(0)
                look_up(0, 0)
                with pe.Fori(0, turns) as i:
                    for u in range(RING):
                        step = i * RING + u
                        acc = bank[6 + u % 2]

                        def add_up(t0, t1):
                            for t in range(t0, t1):
                                t_.matmul(acc[:, 0:w], onehot[:, u, t, :], rows[:, u, t, 0:w], start=(t == 0), stop=False)

                        if n < 2:
                            pe.wait_ge(s.ends, step + 1)
                            t_.transpose(bank[3][:, 0:P], edge_ends[:, u % 2, :], ident[:]).then_inc(s.endsT, 1)
                            pe.wait_ge(s.seqm, step + 1)
                            pe.sem_inc(s_passed, 1)
                            t_.transpose(bank[5][:, 0:HEADS], seq_m[:, 0::2], ident[0:HEADS, 0:HEADS])
                            t_.transpose(bank[5][:, HEADS:2 * HEADS], seq_m[:, 1::2], ident[0:HEADS, 0:HEADS]).then_inc(s.back, 1)
                            pe.wait_ge(s.fac, step + 1)
                            pe.sem_inc(s_passed, 1)
                            t_.matmul(bank[3][0:1, 0:w], fac[:, :], head_rows[:, 0:w], start=True, stop=True)
                        pe.wait_ge(s.sel, step + 1)
                        pe.wait_ge(s.acc, step + 1)
                        if n == 2:
                            pe.wait_ge(s.outw, step + RING)
                        t_.matmul(bank[4][0:1, 0:w], sel[:, u % 2:u % 2 + 1], acc_sb[:, 1 - u % 2, 0:w], start=True, stop=True).then_inc(s.pick, 1)
                        transpose_hot(step + 1)
                        parts = len(DVE_PARTS)
                        pe.wait_ge(s.rhs, step * parts + 1)
                        add_up(*DVE_PARTS[0])
                        look_up(step + 1, (u + 1) % RING)
                        for q in range(1, parts - 1):
                            pe.wait_ge(s.rhs, step * parts + (q + 1))
                            add_up(*DVE_PARTS[q])
                        pe.wait_ge(s.carry, step + 1)
                        t_.matmul(acc[:, 0:w], first_row[0:1, :], carry[0:1, 0:w], start=False, stop=False)
                        pe.wait_ge(s.share, step + 1)
                        add_up(ACT_TILE, ACT_TILE + 1)
                        pe.wait_ge(s.rhs, (step + 1) * parts)
                        t0, t1 = DVE_PARTS[-1]
                        add_up(t0, t1 - 1)
                        t_.matmul(acc[:, 0:w], onehot[:, u, t1 - 1, :], rows[:, u, t1 - 1, 0:w], start=False, stop=True).then_inc(s.done, 1)

            for n in range(3):
                node_pe(n)
                edge_pe(n)

        @block.vector
        def _(dve):
            v = nc.vector
            for n in range(3):
                dve.sem_inc(ns[n].res, 1)
                if n < 2:
                    dve.sem_inc(ns[n].prod, 1)
                dve.sem_inc(es[n].acc, 1)
                dve.sem_inc(es[n].read, 1)
                dve.sem_inc(ns[n].hTs, 2)
            dve.sem_inc(ns[2].copied, 4)
            dve.sem_inc(ns[2].rootr, 1)
            dve.sem_inc(es[2].outw, RING)
            dve.wait_ge(s_const, 1)
            dve.wait_ge(s_wload, 16 * 20)
            nwork = [0]

            def do(ins):
                nwork[0] += 1
                ins.then_inc(s_vplan, 1)
                dve.wait_ge(s_vplan, nwork[0])

            B, E_, NW, CUM, CUX, V = range(6)
            do(v.tensor_copy(ends[:], ends_i[:]))
            do(v.memset(ends[0:1, 0, 0:1], 0.0))
            do(v.tensor_copy(plan[0:1, B, :], ends[0:1, 0, :]))
            do(v.tensor_scalar(plan[0:1, E_, 0:P - 1], ends[0:1, 0, 1:P], -1.0, None, ALU.add))
            do(v.memset(plan[0:1, E_, P - 1:P], float(N_NODES - 1)))
            do(v.tensor_scalar(ends[0:1, 1, :], ends[0:1, 1, :], float(N_NODES - 1), None, ALU.min))
            do(v.tensor_tensor(plan[0:1, E_, :], plan[0:1, E_, :], ends[0:1, 1, :], ALU.max))
            do(v.tensor_tensor(plan_i[0:1, :], plan[0:1, E_, :], plan[0:1, B, :], ALU.subtract))
            do(v.tensor_scalar(plan_i[0:1, :], plan_i[0:1, :], 7, None, ALU.arith_shift_right))
            do(v.tensor_copy(plan[0:1, NW, :], plan_i[0:1, :]))
            do(v.tensor_scalar(plan[0:1, NW, :], plan[0:1, NW, :], 1.0, None, ALU.add))
            do(v.tensor_tensor_scan(plan[0:1, CUM, :], plan[0:1, NW, :], zeros_t[0:1, 0:P], 0.0, ALU.add, ALU.add))
            do(v.tensor_tensor(plan[0:1, CUX, :], plan[0:1, CUM, :], plan[0:1, NW, :], ALU.subtract))
            do(v.tensor_scalar(plan[0:1, V, 0:1], plan[0:1, CUM, P - 1:P], float(RING - 1), None, ALU.add))
            do(v.tensor_copy(turns_i[0:1, 0:1], plan[0:1, V, 0:1]))
            do(v.tensor_scalar(turns_i[0:1, 1:2], turns_i[0:1, 0:1], 2, None, ALU.arith_shift_right))
            v.scalar_tensor_tensor(plan[0:1, V, :], plan[0:1, CUX, :], -float(P), plan[0:1, B, :], ALU.mult, ALU.add).then_inc(s_plan_row, 1)
            dve.wait_ge(s_plan_col, 1)
            do(v.tensor_copy(cols[:], bank[0][:, 0:3]))
            do(v.tensor_scalar(hot[:, 0, :], iota_steps[:], cols[:, 0:1], None, ALU.is_ge))
            do(v.tensor_scalar(hot[:, 1, :], iota_steps[:], cols[:, 1:2], None, ALU.is_ge))
            do(v.tensor_tensor(hot[:, 2, :], hot[:, 1, :], hot[:, 0, :], ALU.subtract))
            v.tensor_scalar(hot[:, 3, :], hot[:, 2, :], cols[:, 2:3], None, ALU.mult).then_inc(s_plan_hot, 1)
            dve.wait_ge(s_plan_sum, 1)
            do(v.tensor_scalar(hot[:, 0, :], iota_steps[:], float(P), -float(N_NODES), ALU.mult, ALU.add))
            do(v.tensor_tensor(hot[:, 0, :], hot[:, 0, :], bank[2][:, 0:MAX_STEPS], ALU.mult))
            do(v.tensor_tensor(hot[:, 0, :], hot[:, 0, :], bank[3][:, 0:MAX_STEPS], ALU.add))
            do(v.tensor_scalar(base_of[:, 1:MAX_STEPS + 1], hot[:, 0, :], float(N_NODES), None, ALU.add))
            do(v.tensor_copy(prev_i[0:1, 1:MAX_STEPS], base_of[0:1, 1:MAX_STEPS]))
            do(v.memset(prev_i[0:1, 0:1], N_NODES))
            do(v.tensor_scalar(step_i[0:1, 0, :], bank[1][0:1, 0:MAX_STEPS], float(P), None, ALU.mult))
            for n in range(2):
                for q in range(2):
                    a_ = att[:, 2 * n + q, :].unsqueeze(1).to_broadcast([P, 2, D])
                    do(v.tensor_tensor(att_tmp[:], wx[n][:, :, 0:D], a_, ALU.mult))
                    do(v.tensor_reduce(wx[n][:, :, D + q * HEADS:D + (q + 1) * HEADS],
                                       att_tmp.rearrange("p k (h d) -> p k h d", h=HEADS), AX.X, ALU.add))
            v.tensor_copy(step_i[0:1, 1, :], base_of[0:1, 1:MAX_STEPS + 1]).then_inc(s_plan, 1)
            dve.wait_ge(s_plan, 1)
            turns = v.value_load(turns_i[0:1, 1:2], min_val=1, max_val=MAX_TURNS)

            def split(t, parts, value, rest, signal=None):
                t.add(v.tensor_copy(parts[:, :, :, 0], value))
                t.settle()
                t.add(v.tensor_tensor(rest, value, parts[:, :, :, 0], ALU.subtract))
                t.settle()
                t.add(v.tensor_copy(parts[:, :, :, 1], rest))
                t.settle()
                t.add(v.tensor_tensor(rest, rest, parts[:, :, :, 1], ALU.subtract))
                t.settle()
                if signal is None:
                    t.add(v.tensor_copy(parts[:, :, :, 2], rest))
                else:
                    v.tensor_copy(parts[:, :, :, 2], rest).then_inc(signal, 1)

            def heads(ap):
                return ap.rearrange("p k (h d) -> p k h d", h=HEADS)

            def node_vec(n):
                s = ns[n]
                n_loads = (1, 2, 3)[n]
                per = (16, 56, 48)[n]

                def scores(t, g, b):
                    sm, own, acc = n_sm[:, b], n_own[:, b], n_acc[:, b]
                    D_EDGE, D_LOOP, E, M, TOP = sm[:, 0], sm[:, 1], sm[:, 4], sm[:, 5], sm[:, 6]
                    dve.wait_ge(s.loaded[b], (g_turn(g) + 1) * (16 * n_loads))
                    t.add(v.tensor_tensor(E, own[:, :, D:D + HEADS], own[:, :, D + HEADS:TABLE], ALU.add))
                    t.add(v.tensor_scalar(M, acc[:, :, ES:MS], 0.0, -BIG, ALU.is_le, ALU.mult))
                    t.settle()
                    t.add(v.scalar_tensor_tensor(E, E, SLOPE, E, ALU.mult, ALU.max))
                    t.add(v.tensor_tensor(M, M, acc[:, :, MS:RS], ALU.add))
                    t.settle()
                    t.add(v.tensor_tensor(E, E, loop_bias[:, bass.ds(g[0] * GROUP, GROUP)].unsqueeze(2).to_broadcast([P, GROUP, HEADS]), ALU.add))
                    t.settle()
                    t.add(v.tensor_tensor(TOP, M, E, ALU.max))
                    t.settle()
                    t.add(v.tensor_tensor(D_EDGE, M, TOP, ALU.subtract))
                    v.tensor_tensor(D_LOOP, E, TOP, ALU.subtract).then_inc(s.dist, 1)

                def combine(t, g, b):
                    sm, own, acc = n_sm[:, b], n_own[:, b], n_acc[:, b]
                    W_EDGE, W_LOOP, DEN = sm[:, 2], sm[:, 3], sm[:, 7]
                    dve.wait_ge(s.wexp, g[0] + 1)
                    t.add(v.tensor_tensor(W_LOOP, W_LOOP, looped[:, bass.ds(g[0] * GROUP, GROUP)].unsqueeze(2).to_broadcast([P, GROUP, HEADS]), ALU.mult))
                    t.add(v.tensor_tensor(DEN, acc[:, :, ES:MS], W_EDGE, ALU.mult))
                    t.settle()
                    t.add(v.tensor_tensor(DEN, DEN, W_LOOP, ALU.add))
                    t.settle()
                    t.add(v.tensor_scalar(DEN, DEN, TINY, None, ALU.max))
                    t.settle()
                    t.add(v.reciprocal(DEN, DEN))
                    t.settle()
                    t.add(v.tensor_tensor(W_EDGE, W_EDGE, DEN, ALU.mult))
                    t.add(v.tensor_tensor(W_LOOP, W_LOOP, DEN, ALU.mult))
                    t.settle()
                    wide = [P, GROUP, HEADS, HID]
                    t.add(v.tensor_tensor(heads(acc[:, :, 0:D]), heads(acc[:, :, 0:D]), W_EDGE.unsqueeze(3).to_broadcast(wide), ALU.mult))
                    t.add(v.tensor_tensor(heads(own[:, :, 0:D]), heads(own[:, :, 0:D]), W_LOOP.unsqueeze(3).to_broadcast(wide), ALU.mult))
                    t.settle()
                    t.add(v.tensor_tensor(acc[:, :, 0:D], acc[:, :, 0:D], own[:, :, 0:D], ALU.add))
                    t.settle()
                    v.tensor_tensor(acc[:, :, 0:D], acc[:, :, 0:D], biases[:, n - 1, :].unsqueeze(1).to_broadcast([P, GROUP, D]),
                                    ALU.add).then_inc(s.conv, 1)

                def counts(t, g, b):
                    cnt, rest = n_cnt[:, b, 0], n_cnt[:, b, 1]
                    t.add(v.tensor_scalar(cnt, n_acc[:, b, :, RS:WIDE], 1.0, None, ALU.max))
                    t.settle()
                    t.add(v.reciprocal(cnt, cnt))
                    t.settle()
                    split(t, n_par[:, b].rearrange("p k (r q) -> p k r q", q=3), cnt, rest)

                def elu(t, g, b):
                    acc, h, xin, st = n_acc[:, b], n_h[:, b], n_x[:, b], n_st[:, b]
                    dve.wait_ge(s.negexp, g[0] + 1)
                    if n == 1:
                        v.scalar_tensor_tensor(h, acc[:, :, 0:D], 0.0, h, ALU.max, ALU.add).then_inc(s.h, 1)
                    else:
                        t.add(v.scalar_tensor_tensor(acc[:, :, 0:D], acc[:, :, 0:D], 0.0, h, ALU.max, ALU.add))
                        t.settle()
                        t.add(v.scalar_tensor_tensor(xin, acc[:, :, 0:D], -1.0, xin, ALU.add, ALU.add))
                        t.settle()

                def variance(t, g, b):
                    xin, st = n_x[:, b], n_st[:, b]
                    if n == 0:
                        dve.wait_ge(s.loaded[b], (g_turn(g) + 1) * (16 * n_loads))
                    for k in range(GROUP):
                        t.add(v.bn_stats(st[:, k, 0:6], xin[:, k, :]))
                    t.settle()
                    dve.sem_inc(s_passed, 1)
                    for k in range(GROUP):
                        last = v.bn_aggr(st[:, k, 6:8], st[:, k, 0:6])
                    last.then_inc(s.var, 1)

                def normalise(t, g, b):
                    xin, st, h = n_x[:, b], n_st[:, b], n_h[:, b]
                    dve.wait_ge(s.std, g[0] + 1)
                    t.add(v.reciprocal(st[:, :, 9:10], st[:, :, 8:9]))
                    t.settle()
                    for k in range(GROUP):
                        last = v.tensor_scalar(h[:, k, :], xin[:, k, :], st[:, k, 6:7], st[:, k, 9:10], ALU.subtract, ALU.mult)
                    last.then_inc(s.h, 1)

                def results(t, g, b):
                    o = n_out[:, b]
                    if n < 2:
                        dve.wait_ge(s.prod, g[0] + 2)
                        split(t, n_adp[:, b].rearrange("p k (h q) -> p k h q", q=3), o[:, :, D + HEADS:TABLE], n_sm[:, b, 8], s.res)
                    else:
                        xin = n_x[:, b]
                        t.add(v.tensor_tensor(xin, xin, biases[:, 2, :].unsqueeze(1).to_broadcast([P, GROUP, D]), ALU.add))
                        t.settle()
                        for k in range(GROUP):
                            dve.wait_ge(s.mm, g[0] * (5 * GROUP) + 5 * (k + 1))
                            last = v.tensor_tensor(o[:, k, 0:D], xin[:, k, :], bank[6][:, 0:D], ALU.add).then_inc(s.rootr, 1)
                        dve.wait_ge(s.rootr, g[0] * GROUP + (GROUP + 1))
                        dve.sem_inc(s.res, 1)

                def g_turn(g):
                    return g[1]

                with dve.Fori(0, NODE_TURNS) as i:
                    t = Turn(dve, s.vec, per, i)
                    first, second = (i * HALVES, i), (i * HALVES + 1, i)
                    if n == 0:
                        variance(t, first, 0)
                        variance(t, second, 1)
                        normalise(t, first, 0)
                        normalise(t, second, 1)
                        results(t, first, 0)
                        results(t, second, 1)
                    elif n == 1:
                        scores(t, first, 0)
                        counts(t, first, 0)
                        combine(t, first, 0)
                        scores(t, second, 1)
                        counts(t, second, 1)
                        elu(t, first, 0)
                        combine(t, second, 1)
                        results(t, first, 0)
                        elu(t, second, 1)
                        results(t, second, 1)
                    else:
                        scores(t, first, 0)
                        combine(t, first, 0)
                        scores(t, second, 1)
                        elu(t, first, 0)
                        variance(t, first, 0)
                        combine(t, second, 1)
                        normalise(t, first, 0)
                        elu(t, second, 1)
                        variance(t, second, 1)
                        normalise(t, second, 1)
                        results(t, first, 0)
                        results(t, second, 1)
                    t.end()

            HT = [P, HEADS, TILES]

            def over_heads(ap):
                return ap.unsqueeze(1).to_broadcast(HT)

            def over_tiles(ap):
                return ap.unsqueeze(2).to_broadcast(HT)

            def edge_vec(n):
                s = es[n]
                w = width[n]
                per_prep = (8, 7, 1)[n]
                per_vec = (11, 11, 3)[n]
                L = HEADS * (TILES + 1)

                def prepare(step, u, turn):
                    t = Turn(dve, s.prep, per_prep, step)
                    kf = keyf[:, u, :]
                    base = base_of[:, bass.ds(step + 1, 1)]
                    dve.wait_ge(s.loaded[u], (turn + 1) * (16 * edge_loads_per_step[n]))
                    t.add(v.tensor_scalar(kf, key_i[:, u, :], base, None, ALU.subtract))
                    t.settle()
                    v.tensor_tensor(onehot[:, u, :, :], kf[:, 1:TILES + 1].unsqueeze(2).to_broadcast([P, TILES, P]),
                                    iota_win[:].unsqueeze(1).to_broadcast([P, TILES, P]), ALU.is_equal).then_inc(s.hot, 1)
                    v.tensor_scalar(sel[:, u % 2:u % 2 + 1], iota_part[:], base_of[:, bass.ds(step, 1)], base,
                                    ALU.add, ALU.is_equal).then_inc(s.sel, 1)
                    if n < 2:
                        df = differ[:, u % 2, :]
                        t.add(v.tensor_tensor(df, kf[:, 1:KEYS], kf[:, 0:KEYS - 1], ALU.not_equal))
                        t.add(v.tensor_scalar(edge_ends[:, u % 2, 96:96 + HEADS], kf[:, TILES:TILES + 1].to_broadcast([P, HEADS]),
                                              kf[:, 1:2], -BIG, ALU.not_equal, ALU.mult))
                        t.add(v.tensor_scalar(not_first[:, u % 2, :], kf[:, 1:TILES + 1], kf[:, 1:2], -BIG, ALU.not_equal, ALU.mult))
                        t.add(v.tensor_scalar(not_final[:, u % 2, :], kf[:, 1:TILES + 1], kf[:, TILES:TILES + 1], -BIG, ALU.not_equal, ALU.mult))
                        if n == 0:
                            t.add(v.tensor_tensor(rows[:, u, :, RS:WIDE], typ_i[:, u, :].unsqueeze(2).to_broadcast([P, TILES, N_REL]),
                                                  iota_rel[:].unsqueeze(1).to_broadcast([P, TILES, N_REL]), ALU.is_equal))
                        t.settle()
                        t.add(v.tensor_scalar(by_head(cut[:, u % 2, 0:L])[:, :, 1:TILES],
                                              df[:, 1:TILES].unsqueeze(1).to_broadcast([P, HEADS, TILES - 1]), -BIG, None, ALU.mult))
                        t.add(v.tensor_scalar(edge_ends[:, u % 2, 64:64 + HEADS], df[:, 0:1].to_broadcast([P, HEADS]), -BIG, None, ALU.mult))
                    t.end()

                def row_numbers(u, turn):
                    dve.wait_ge(s.loaded[u], (turn + 1) * (16 * edge_loads_per_step[n]))
                    v.scalar_tensor_tensor(row_i[:, u, :], src_i[:, u, :], float(N_REL), typ_i[:, u, :],
                                           ALU.mult, ALU.add).then_inc(s.idx, 1)

                def out_window(step, u):
                    dve.wait_ge(s.acc, step + 2)
                    v.tensor_tensor(out_sb[:, u % 2, :], bank[6 + u % 2][:, 0:D], win_root[:, u, :], ALU.add).then_inc(s.outw, 1)

                if n == 2:
                    row_numbers(0, 0)
                    row_numbers(1, 0)
                    v.memset(bank[7][:, 0:D], 0.0).then_inc(s_cleared, 1)
                    dve.wait_ge(s_cleared, 1)
                prepare(0, 0, 0)
                with dve.Fori(0, turns) as i:
                    for u in range(RING):
                        step = i * RING + u
                        t = Turn(dve, s.vec, per_vec, step)
                        turn = i if u + 1 < RING else i + 1

                        def go(ins):
                            t.add(ins)
                            t.settle()

                        if n < 2:
                            df, cu = differ[:, u % 2, :], cut[:, u % 2, :]
                            dve.wait_ge(s.dstv, step + 1)
                            v.tensor_reduce(z[:], bank[2][:, 0:TILES * 3 * HEADS].rearrange("p (t h q) -> p t h q", h=HEADS, q=3),
                                            AX.X, ALU.add).then_inc(s.read, 1)
                            dve.wait_ge(s.read, step + 2)
                            dve.wait_ge(s.gathered[u], (i + 1) * (16 * TILES))
                            go(v.tensor_tensor(zz.rearrange("p h t -> p t h"), z[:], rows[:, u, :, D:D + HEADS], ALU.add))
                            scv = by_head(sc[:, :])[:, :, 0:TILES]
                            go(v.scalar_tensor_tensor(scv, zz[:], SLOPE, zz[:], ALU.mult, ALU.max))
                            go(v.tensor_tensor_scan(run_f[:], cu[:, 0:L], sc[:], -BIG, ALU.add, ALU.max))
                            go(v.tensor_tensor_scan(run_m[:, ::-1], cu[:, L:0:-1], run_f[:, ::-1], -BIG, ALU.add, ALU.max))
                            rm = by_head(run_m[:, :])[:, :, 0:TILES]
                            t.add(v.tensor_copy(edge_ends[:, u % 2, 0:HEADS], rm[:, :, 0]))
                            v.tensor_copy(edge_ends[:, u % 2, 32:32 + HEADS], rm[:, :, TILES - 1]).then_inc(s.ends, 1)
                            prepare(step + 1, (u + 1) % RING, turn)
                            dve.wait_ge(s.seq, step + 1)
                            before = seq_f[:, 1 - u % 2, 2 * P - 1:2 * P]
                            go(v.tensor_tensor_scan(seq_f[:, u % 2, :], seq_c[:, 0:2 * P], seq_v[:], before, ALU.add, ALU.max))
                            v.tensor_tensor_scan(seq_m[:, ::-1], seq_c[:, 2 * P:0:-1], seq_f[:, u % 2, ::-1], -BIG, ALU.add, ALU.max).then_inc(s.seqm, 1)
                            dve.wait_ge(s.seqm, step + 1)
                            v.tensor_scalar(fac_d[:], before, seq_m[:, 0:1], 0.0, ALU.subtract, ALU.min).then_inc(s.facd, 1)
                            dve.wait_ge(s.back, step + 1)
                            tm = by_head(tmp_m[:, :])[:, :, 0:TILES]
                            tn = tmp_n[:]
                            t.add(v.tensor_tensor(tm, over_tiles(bank[5][:, 0:HEADS]), over_heads(not_first[:, u % 2, :]), ALU.add))
                            go(v.tensor_tensor(tn, over_tiles(bank[5][:, HEADS:2 * HEADS]), over_heads(not_final[:, u % 2, :]), ALU.add))
                            go(v.tensor_tensor(tm, tm, tn, ALU.max))
                            go(v.tensor_tensor(rm, rm, tm, ALU.max))
                            v.tensor_tensor(zz[:], scv, rm, ALU.subtract).then_inc(s.expd, 1)
                            t.add(v.tensor_tensor(rows[:, u, :, MS:RS], by_head(run_m[:, :]).rearrange("p h t -> p t h")[:, 0:TILES, :],
                                                  df[:, 1:TILES + 1].unsqueeze(2).to_broadcast([P, TILES, HEADS]), ALU.mult))
                            t.settle()
                            dve.wait_ge(s.exp, step + 1)
                            for q, (t0, t1) in enumerate(DVE_PARTS):
                                r = rows[:, u, t0:t1, 0:D].rearrange("p t (h d) -> p t h d", h=HEADS)
                                v.tensor_tensor(r, r, rows[:, u, t0:t1, ES:MS].unsqueeze(3).to_broadcast([P, t1 - t0, HEADS, HID]),
                                                ALU.mult).then_inc(s.rhs, 1)
                                if q == 0:
                                    dve.wait_ge(s.facr, step + 1)
                                    v.tensor_tensor(carry[:, 0:w], fac_row[:, 0:w], bank[4][0:1, 0:w], ALU.mult).then_inc(s.carry, 1)
                        else:
                            co = coef[:, u % 2, :]
                            row_numbers((u + 2) % RING, i if u + 2 < RING else i + 1)
                            go(v.tensor_tensor(typ_hot[:], typ_i[:, u, :].unsqueeze(2).to_broadcast([P, TILES, N_REL]),
                                               iota_rel[:].unsqueeze(1).to_broadcast([P, TILES, N_REL]), ALU.is_equal))
                            dve.wait_ge(s.dstv, step + 1)
                            v.tensor_reduce(ic[:], bank[2][:, 0:TILES * 3 * N_REL].rearrange("p (t r q) -> p t r q", r=N_REL, q=3),
                                            AX.X, ALU.add).then_inc(s.read, 1)
                            dve.wait_ge(s.read, step + 2)
                            go(v.tensor_tensor(ic[:], ic[:], typ_hot[:], ALU.mult))
                            go(v.tensor_reduce(co, ic[:], AX.X, ALU.add))
                            v.tensor_tensor(co, co, wts[:, u, :], ALU.mult).then_inc(s.coef, 1)
                            prepare(step + 1, (u + 1) % RING, turn)
                            dve.wait_ge(s.coef, step + 1)
                            dve.wait_ge(s.gathered[u], (i + 1) * (16 * TILES))
                            for q, (t0, t1) in enumerate(DVE_PARTS):
                                r = rows[:, u, t0:t1, 0:D]
                                v.tensor_tensor(r, r, co[:, t0:t1].unsqueeze(2).to_broadcast([P, t1 - t0, D]), ALU.mult).then_inc(s.rhs, 1)
                                if q == 0:
                                    dve.wait_ge(s.pick, step + 1)
                                    v.tensor_copy(carry[0:1, 0:D], bank[4][0:1, 0:D]).then_inc(s.carry, 1)
                                    out_window(step - 1, (u - 1) % RING)
                        t.end()
                if n == 2:
                    out_window(turns * RING - 1, RING - 1)

            for n in range(3):
                node_vec(n)
                edge_vec(n)


def kernel(**inputs):
    import numpy as _np
    import concourse.bacc as _bacc
    from concourse import mybir as _mybir
    from concourse.bass_utils import run_bass_kernel_spmd as _run

    a = {k: _np.ascontiguousarray(v) for k, v in inputs.items()}
    pad = (N_CHUNKS + 1) * CHUNK - N_EDGES

    def padded(v, value):
        return _np.concatenate([v, _np.full(pad, value, v.dtype)])

    def in_partitions(v):
        return v.reshape(-1, TILES)

    keys = padded(a["dst"], PAD_KEY)
    before = _np.concatenate([_np.full(1, -1, keys.dtype), keys])[:-1]
    after = _np.concatenate([keys, _np.full(1, PAD_KEY, keys.dtype)])[1:]
    host = {
        "x": _np.concatenate([a["x"], _np.zeros((NP - N_NODES, D), a["x"].dtype)]),
        "edge_records": _np.concatenate([
            in_partitions(before)[:, :1], in_partitions(keys), in_partitions(after)[:, -1:],
            in_partitions(padded(a["src"], 0)), in_partitions(padded(a["edge_type_8"], 0))], axis=1),
        "chunk_firsts": keys[None, 0:N_CHUNKS * CHUNK:CHUNK],
        "chunk_lasts": keys[None, CHUNK - 1:N_CHUNKS * CHUNK:CHUNK],
        "edge_weight": in_partitions(padded(a["edge_weight"], 0)),
    }
    for k in ("W1", "att_src1", "att_dst1", "b1", "W2", "att_src2", "att_dst2", "b2"):
        host[k] = a["L0_gnn_" + k]
    for k in ("weight", "root", "bias"):
        host[k] = a["L1_gnn_" + k]

    nc = _bacc.Bacc("TRN2", target_bir_lowering=False, num_devices=1)
    arrays, args = {}, []
    for name, v in host.items():
        arrays[f"in_{name}"] = v = _np.ascontiguousarray(v)
        args.append(nc.dram_tensor(f"in_{name}", v.shape, _mybir.dt.from_np(v.dtype), kind="ExternalInput").ap())
    args.append(nc.dram_tensor("out_0", (NP, D), _mybir.dt.float32, kind="ExternalOutput").ap())
    build(nc, *args)
    r = _run(nc, [arrays], core_ids=[0])
    return r.results[0]["out_0"][:N_NODES]
```

```python
import concourse.bass as bass
from concourse import mybir
from contextlib import ExitStack

F32 = mybir.dt.float32
BF16 = mybir.dt.bfloat16
I32 = mybir.dt.int32
ALU = mybir.AluOpType
ACT = mybir.ActivationFunctionType
AX = mybir.AxisListType

P = 128
N_NODES = 12500
N_EDGES = 212500
N_LOOPED = 6250
D = 256
HEADS = 4
HID = 64
N_REL = 8
SLOPE = 0.2
EPS = 1e-5
BIG = 1e30
TINY = 1e-30

TILES = 13
CHUNK = TILES * P
N_CHUNKS = -(-N_EDGES // CHUNK)
GROUP = 3
HALVES = 2
NODE_GROUPS = -(-(N_NODES + P) // (P * GROUP))
NODE_TURNS = (NODE_GROUPS - 1) // HALVES
NODE_TILES = NODE_GROUPS * GROUP
LOOPED_TURNS = -(-(-(-N_LOOPED // (P * GROUP)) - 1) // HALVES)
NP = NODE_TILES * P
TAIL = N_NODES // P
RING = 4
DVE_PARTS = ((0, 4), (4, 8), (8, TILES - 1))
ACT_TILE = TILES - 1
MAX_TURNS = -(-(N_CHUNKS + N_NODES // P) // RING)
MAX_STEPS = (MAX_TURNS + 2) * RING
PAD_KEY = 1 << 20
KEYS = TILES + 2
RECORD = KEYS + 2 * TILES

TABLE = D + 2 * HEADS
ES, MS, RS = D, D + HEADS, D + 2 * HEADS
WIDE = TABLE + N_REL


class Turn:

    def __init__(self, engine, sem, per_turn, turn, before=0):
        self.engine, self.sem, self.per_turn, self.turn, self.count = engine, sem, per_turn, turn, 0
        self.before = before

    def add(self, instruction):
        instruction.then_inc(self.sem, 1)
        self.count += 1

    def settle(self):
        self.engine.wait_ge(self.sem, self.turn * self.per_turn + (self.before + self.count))

    def end(self):
        assert self.count == self.per_turn, (self.count, self.per_turn)


def build(nc, x, records, firsts, lasts, ewt, W1, as1, ad1, b1, W2, as2, ad2, b2, Wr, root, rbias, out):
    assert N_CHUNKS == P

    def dram(name, shape, dt):
        return nc.dram_tensor(name, shape, dt, kind="Internal").ap()

    tables = [dram("node_rows_1", (NP, TABLE), F32), dram("node_rows_2", (NP, TABLE), F32)]
    ads = [dram("a_dst_parts_1", (NP, 3 * HEADS), BF16), dram("a_dst_parts_2", (NP, 3 * HEADS), BF16)]
    accs = [dram("edge_sums_1", (NP, WIDE), F32), dram("edge_sums_2", (NP, WIDE), F32)]
    yrel = dram("relation_rows", (NP, N_REL * D), F32)
    resd = dram("residual_rows", (NP, D), F32)
    hTd = dram("h_transposed", (D, NP), F32).rearrange("(c p) n -> p c n", p=P)
    yrows = yrel.rearrange("n (r d) -> (n r) d", r=N_REL)

    ctx = ExitStack()
    with ctx:
        def sb(name, shape, dt=F32):
            return ctx.enter_context(nc.sbuf_tensor(name, shape, dt))

        def sem(name):
            return ctx.enter_context(nc.semaphore(name))

        psum = ctx.enter_context(nc.psum_tensor("psum", [P, 8, 512], F32))
        bank = [psum[:, i, :] for i in range(8)]

        ident = sb("ident", [P, P])
        identb = sb("identb", [P, P], BF16)
        ones = sb("ones", [P, P])
        iota_win = sb("iota_win", [P, P])
        iota_part = sb("iota_part", [P, 1])
        iota_steps = sb("iota_steps", [P, MAX_STEPS])
        iota_rel = sb("iota_rel", [P, N_REL])
        eps_t = sb("eps_t", [P, 1])
        minus_one = sb("minus_one", [P, 1])
        head_rows = sb("head_rows", [HEADS + 1, WIDE])
        first_row = sb("first_row", [1, P])
        node_no = sb("node_no", [P, NODE_TILES])
        looped = sb("looped", [P, NODE_TILES])
        loop_bias = sb("loop_bias", [P, NODE_TILES])

        ends_i = sb("ends_i", [1, 2, P], I32)
        ends = sb("ends", [1, 2, P])
        plan = sb("plan", [1, 6, P])
        plan_i = sb("plan_i", [1, P], I32)
        cols = sb("cols", [P, 3])
        hot = sb("hot", [P, 4, MAX_STEPS])
        base_of = sb("base_of", [P, MAX_STEPS + 1])
        step_i = sb("step_i", [1, 2, MAX_STEPS], I32)
        prev_i = sb("prev_i", [1, MAX_STEPS], I32)
        turns_i = sb("turns_i", [1, 2], I32)

        wx = [sb("w1x", [P, 2, TABLE]), sb("w2x", [P, 2, TABLE])]
        att = sb("att", [P, 4, D])
        att_tmp = sb("att_tmp", [P, 2, D])
        biases = sb("biases", [P, 3, D])
        wrel = sb("wrel", [P, 2, N_REL + 1, D])

        shared = sb("shared", [P, RING * TILES * WIDE])
        rows = shared[:, :].rearrange("p (u t w) -> p u t w", u=RING, t=TILES)
        taken = [0]

        def shared_buffer(*shape):
            n = 1
            for q in shape:
                n *= q
            taken[0] += n
            assert taken[0] <= RING * TILES * WIDE
            flat = shared[:, taken[0] - n:taken[0]]
            if len(shape) == 2:
                return flat.rearrange("p (b d) -> p b d", b=shape[0])
            return flat.rearrange("p (b k d) -> p b k d", b=shape[0], k=shape[1])

        n_x = shared_buffer(HALVES, GROUP, D)
        n_own = shared_buffer(HALVES, GROUP, TABLE)
        n_acc = shared_buffer(HALVES, GROUP, WIDE)
        n_st = sb("n_st", [P, HALVES, GROUP, 10])
        n_h = shared_buffer(HALVES, GROUP, D)
        n_neg = shared_buffer(HALVES, GROUP, D)
        n_hT = sb("n_hT", [P, 2, 2, P])
        n_out = shared_buffer(HALVES, GROUP, TABLE)
        n_y = shared_buffer(2, N_REL * D)
        n_adp = sb("n_adp", [P, HALVES, GROUP, 3 * HEADS], BF16)
        n_sm = sb("n_sm", [P, HALVES, 12, GROUP, HEADS])

        record = sb("record", [P, RING, RECORD], I32)
        key_i = record[:, :, 0:KEYS]
        src_i = record[:, :, KEYS:KEYS + TILES]
        typ_i = record[:, :, KEYS + TILES:RECORD]
        row_i = sb("row_i", [P, RING, TILES], I32)
        wts = sb("wts", [P, RING, TILES])
        keyf = sb("keyf", [P, RING, KEYS])
        win_ad = sb("win_ad", [P, RING, 3 * HEADS], BF16)
        win_ic = sb("win_ic", [P, RING, 3 * N_REL], BF16)
        win_cnt = sb("win_cnt", [P, RING, N_REL])
        cnt_rest = sb("cnt_rest", [P, 2, N_REL])
        win_res = sb("win_res", [P, RING, D])
        win_hT = sb("win_hT", [P, RING, 2, P])
        onehot = sb("onehot", [P, RING, TILES, P])
        onehot_b = sb("onehot_b", [P, TILES, P], BF16)
        onehot_T = sb("onehot_T", [P, TILES, P], BF16)
        differ = sb("differ", [P, 2, TILES + 1])
        cut = sb("cut", [P, 2, HEADS * (TILES + 1) + 1])
        sc = sb("sc", [P, HEADS * (TILES + 1)])
        run_f = sb("run_f", [P, HEADS * (TILES + 1)])
        run_m = sb("run_m", [P, HEADS * (TILES + 1)])
        tmp_m = sb("tmp_m", [P, HEADS * (TILES + 1)])
        tmp_n = sb("tmp_n", [P, HEADS, TILES])
        z = sb("z", [P, TILES, HEADS])
        zz = sb("zz", [P, HEADS, TILES])
        not_first = sb("not_first", [P, 2, TILES])
        not_final = sb("not_final", [P, 2, TILES])
        edge_ends = sb("edge_ends", [P, 2, P])
        seq_v = sb("seq_v", [HEADS, 2 * P])
        seq_c = sb("seq_c", [HEADS, 2 * P + 1])
        seq_f = sb("seq_f", [HEADS, 2, 2 * P])
        seq_m = sb("seq_m", [HEADS, 2 * P])
        fac_d = sb("fac_d", [HEADS, 1])
        fac = sb("fac", [HEADS + 1, 1])
        fac_row = sb("fac_row", [1, WIDE])
        carry = sb("carry", [1, WIDE])
        sel = sb("sel", [P, RING])
        acc_sb = sb("acc_sb", [P, 2, WIDE])
        out_sb = sb("out_sb", [P, 2, D])
        typ_hot = sb("typ_hot", [P, TILES, N_REL])
        ic = sb("ic", [P, TILES, N_REL])
        coef = sb("coef", [P, 2, TILES])
        zeros_t = sb("zeros_t", [P, WIDE])

        s_const = sem("s_const")
        s_ends = sem("s_ends")
        s_wload = sem("s_wload")
        s_rload = sem("s_rload")
        s_vplan = sem("s_vplan")
        s_plan_row = sem("s_plan_row")
        s_plan_col = sem("s_plan_col")
        s_plan = sem("s_plan")
        s_zeroed = sem("s_zeroed")
        s_prepared = sem("s_prepared")
        s_pool = sem("s_pool")
        s_passed = sem("s_passed")

        class NodeSems:

            def __init__(self, n):
                self.loaded = [sem(f"n{n}_loaded{b}") for b in range(HALVES)]
                self.stored = [sem(f"n{n}_stored{b}") for b in range(HALVES)]
                self.vec = sem(f"n{n}_vec")
                if n > 0:
                    self.dist = sem(f"n{n}_dist")
                    self.wexp = sem(f"n{n}_wexp")
                    self.conv = sem(f"n{n}_conv")
                    self.neg = sem(f"n{n}_neg")
                    self.negexp = sem(f"n{n}_negexp")
                if n != 1:
                    self.var = sem(f"n{n}_var")
                    self.std = sem(f"n{n}_std")
                self.h = sem(f"n{n}_h")
                self.hT = sem(f"n{n}_hT")
                self.hTs = sem(f"n{n}_hTs")
                self.mm = sem(f"n{n}_mm")
                self.res = sem(f"n{n}_res")
                if n < 2:
                    self.prod = sem(f"n{n}_prod")
                else:
                    self.copied = sem("n2_copied")
                    self.ystored = [sem(f"n2_ystored{y}") for y in range(2)]

        class EdgeSems:

            def __init__(self, n):
                self.loaded = [sem(f"e{n}_loaded{u}") for u in range(RING)]
                self.gathered = [sem(f"e{n}_gathered{u}") for u in range(RING)]
                self.stored = sem(f"e{n}_stored")
                self.prep = sem(f"e{n}_prep")
                self.vec = sem(f"e{n}_vec")
                self.hot = sem(f"e{n}_hot")
                self.hotb = sem(f"e{n}_hotb")
                self.hotT = sem(f"e{n}_hotT")
                self.hotTs = sem(f"e{n}_hotTs")
                self.dstv = sem(f"e{n}_dstv")
                self.sel = sem(f"e{n}_sel")
                self.pick = sem(f"e{n}_pick")
                self.carry = sem(f"e{n}_carry")
                self.read = sem(f"e{n}_read")
                self.rhs = sem(f"e{n}_rhs")
                self.share = sem(f"e{n}_share")
                self.done = sem(f"e{n}_done")
                self.acc = sem(f"e{n}_acc")
                if n < 2:
                    self.ends = sem(f"e{n}_ends")
                    self.endsT = sem(f"e{n}_endsT")
                    self.seq = sem(f"e{n}_seq")
                    self.seqm = sem(f"e{n}_seqm")
                    self.back = sem(f"e{n}_back")
                    self.facd = sem(f"e{n}_facd")
                    self.fac = sem(f"e{n}_fac")
                    self.facr = sem(f"e{n}_facr")
                    self.expd = sem(f"e{n}_expd")
                    self.exp = sem(f"e{n}_exp")
                else:
                    self.coef = sem(f"e{n}_coef")
                    self.idx = sem(f"e{n}_idx")
                    self.outp = sem("e2_outp")
                    self.outw = sem(f"e{n}_outw")

        ns = [NodeSems(n) for n in range(3)]
        es = [EdgeSems(n) for n in range(3)]

        block = ctx.enter_context(nc.Block())

        def by_head(t, n=TILES + 1, part=P):
            return t.rearrange("p (h t) -> p h t", h=HEADS)

        x_v = x.rearrange("(j p) d -> j p d", p=P)

        def over_groups(engine, body, n):
            looped_turns = LOOPED_TURNS if n > 0 else 0
            for start, stop in ((0, looped_turns), (looped_turns, NODE_TURNS)):
                if stop > start:
                    with engine.Fori(start, stop) as i:
                        for b in range(HALVES):
                            body(i * HALVES + b, i, b, True, start < looped_turns)
            for g in range(NODE_TURNS * HALVES, NODE_GROUPS):
                body(g, NODE_TURNS, g % HALVES, g + 1 < NODE_GROUPS, False)

        n_stores = (2, 2, 1)
        edge_loads_per_step = (2, 2, 5)
        prep_steps = (8, 7, 8)
        loads_ahead = (3, 3, 2)
        width = (WIDE, TABLE, D)

        def group_rows(ap, g):
            return ap[bass.ds(g * (GROUP * P), GROUP * P), :].rearrange("(k p) d -> p k d", p=P)

        def tile_rows(ap, j):
            return ap[bass.ds(j * P, P), :]

        @block.sync
        def _(sp):
            sp.dma_start(ends_i[0:1, 0, :], firsts).then_inc(s_ends, 16)
            sp.dma_start(ends_i[0:1, 1, :], lasts).then_inc(s_ends, 16)
            for t, W in ((wx[0], W1), (wx[1], W2)):
                sp.dma_start(t[:, :, 0:D], W.rearrange("(k p) n -> p k n", p=P)).then_inc(s_wload, 16)
            for q, a in enumerate((as1, ad1, as2, ad2)):
                sp.dma_start(att[:, q, :], a.rearrange("h d -> (h d)").partition_broadcast(P)).then_inc(s_wload, 16)
            for q, b in enumerate((b1, b2, rbias)):
                sp.dma_start(biases[:, q, :], b.partition_broadcast(P)).then_inc(s_wload, 16)
            sp.wait_ge(s_const, 1)
            for a in accs:
                for j in range(TAIL, NODE_TILES):
                    sp.dma_start(a[j * P:(j + 1) * P, :], zeros_t[:, :]).then_inc(s_zeroed, 16)

            def node_loads(n):
                s = ns[n]

                def load(g, b, loops):
                    sp.wait_ge(s.h, g + 1)
                    if n != 1:
                        sp.dma_start(n_x[:, b, :, :], group_rows(x, g)).then_inc(s.loaded[b], 16)
                    if n > 0:
                        sp.dma_start(n_acc[:, b, :, 0:TABLE],
                                     group_rows(accs[n - 1], g)[:, :, 0:TABLE]).then_inc(s.loaded[b], 16)
                    if loops:
                        sp.dma_start(n_own[:, b, :, :], group_rows(tables[n - 1], g)).then_inc(s.loaded[b], 16)

                def store(g, b):
                    sp.wait_ge(s.res, g + 1)
                    if n < 2:
                        sp.dma_start(group_rows(tables[n], g), n_out[:, b, :, :]).then_inc(s.stored[b], 16)
                        sp.dma_start(group_rows(ads[n], g), n_adp[:, b, :, :]).then_inc(s.stored[b], 16)
                    else:
                        sp.dma_start(group_rows(resd, g), n_out[:, b, :, 0:D]).then_inc(s.stored[b], 16)

                for b in range(HALVES):
                    load(b, b, n > 0)
                if n == 0:
                    for r in range(N_REL):
                        sp.dma_start(wrel[:, :, r, :], Wr[r].rearrange("(k p) n -> p k n", p=P)).then_inc(s_rload, 16)
                    sp.dma_start(wrel[:, :, N_REL, :], root.rearrange("(k p) n -> p k n", p=P)).then_inc(s_rload, 16)
                looped_turns = LOOPED_TURNS if n > 0 else 0
                for start, stop in ((0, looped_turns), (looped_turns, NODE_TURNS - 1)):
                    if stop > start:
                        with sp.Fori(start, stop) as i:
                            for b in range(HALVES):
                                load(i * HALVES + (b + HALVES), b, start < looped_turns)
                                store(i * HALVES + b, b)
                for g in range((NODE_TURNS - 1) * HALVES, NODE_GROUPS):
                    if g + HALVES < NODE_GROUPS:
                        load(g + HALVES, g % HALVES, False)
                    store(g, g % HALVES)

            def edge_loads(n):
                s = es[n]

                def load(step, u):
                    r0 = nc.sync.value_load(step_i[0:1, 0, bass.ds(step, 1)], min_val=0, max_val=N_CHUNKS * P)
                    b0 = nc.sync.value_load(step_i[0:1, 1, bass.ds(step, 1)], min_val=0, max_val=N_NODES)
                    if n < 2:
                        sp.wait_ge(s.done, step + 1)
                    else:
                        sp.wait_ge(s.outw, step + 2)
                    sp.dma_start(record[:, u, :], records[bass.ds(r0, P), :]).then_inc(s.loaded[u], 16)
                    if n < 2:
                        sp.dma_start(win_ad[:, u, :], ads[n][bass.ds(b0, P), :]).then_inc(s.loaded[u], 16)
                    else:
                        sp.dma_start(wts[:, u, :], ewt[bass.ds(r0, P), :]).then_inc(s.loaded[u], 16)
                        sp.dma_start(win_cnt[:, u, :], accs[0][bass.ds(b0, P), RS:WIDE]).then_inc(s.loaded[u], 16)
                        sp.dma_start(win_res[:, u, :], resd[bass.ds(b0, P), :]).then_inc(s.loaded[u], 16)
                        sp.dma_start(win_hT[:, u, :, :], hTd[:, :, bass.ds(b0, P)]).then_inc(s.loaded[u], 16)

                ahead = loads_ahead[n]
                for step in range(ahead):
                    load(step, step)
                with sp.Fori(0, turns) as i:
                    for u in range(RING):
                        load(i * RING + (u + ahead), (u + ahead) % RING)

            for n in range(3):
                node_loads(n)
                for b in range(HALVES):
                    sp.wait_ge(ns[n].stored[b], 16 + len(range(b, NODE_GROUPS, HALVES)) * 16 * n_stores[n])
                if n == 2:
                    for y in range(2):
                        sp.wait_ge(ns[n].ystored[y], 16 + len(range(y, NODE_TILES, 2)) * 32)
                if n == 0:
                    sp.wait_ge(s_zeroed, 2 * 16 * (NODE_TILES - TAIL))
                    sp.wait_ge(s_plan, 1)
                    turns = nc.sync.value_load(turns_i[0:1, 1:2], min_val=1, max_val=MAX_TURNS)
                edge_loads(n)
                sp.wait_ge(es[n].stored, turns * (16 * RING) + (16 if n < 2 else 32))
                if n < 2:
                    sp.wait_ge(s_prepared, n + 1)
                sp.sem_inc(s_passed, 1)


        @block.gpsimd
        def _(pool):
            g = nc.gpsimd
            g.memset(ident[:], 0.0)
            g.memset(identb[:], 0.0)
            g.memset(ones[:], 1.0)
            g.memset(eps_t[:], EPS)
            g.memset(minus_one[:], -1.0)
            g.memset(win_res[:], 0.0)
            g.memset(zeros_t[:], 0.0)
            g.memset(acc_sb[:], 0.0)
            g.memset(edge_ends[:], 0.0)
            g.memset(cut[:], -BIG)
            g.memset(sc[:], -BIG)
            g.memset(seq_c[:], 0.0)
            g.memset(seq_f[:], -BIG)
            g.memset(fac[:], 1.0)
            g.memset(first_row[:], 0.0)
            g.memset(base_of[:], -4.0 * PAD_KEY)
            g.memset(head_rows[:], 0.0)
            g.iota(iota_win[:], [[1, P]], base=0, channel_multiplier=0, allow_small_or_imprecise_dtypes=True)
            g.iota(iota_part[:], [[0, 1]], base=0, channel_multiplier=1, allow_small_or_imprecise_dtypes=True)
            g.iota(iota_steps[:], [[1, MAX_STEPS]], base=0, channel_multiplier=0, allow_small_or_imprecise_dtypes=True)
            g.iota(iota_rel[:], [[1, N_REL]], base=0, channel_multiplier=0, allow_small_or_imprecise_dtypes=True)
            g.iota(node_no[:], [[P, NODE_TILES]], base=0, channel_multiplier=1,
                   allow_small_or_imprecise_dtypes=True).then_inc(s_pool, 1)
            pool.wait_ge(s_pool, 1)
            g.memset(first_row[0:1, 0:1], 1.0)
            g.affine_select(out=ident[:], in_=ident[:], compare_op=ALU.not_equal, fill=1.0, base=0,
                            pattern=[[-1, P]], channel_multiplier=1)
            g.affine_select(out=identb[:], in_=identb[:], compare_op=ALU.not_equal, fill=1.0, base=0,
                            pattern=[[-1, P]], channel_multiplier=1)
            g.affine_select(out=head_rows[:, 0:D], in_=head_rows[:, 0:D], compare_op=ALU.not_equal, fill=1.0, base=0,
                            pattern=[[-1, HEADS], [0, HID]], channel_multiplier=1)
            g.affine_select(out=head_rows[:, ES:MS], in_=head_rows[:, ES:MS], compare_op=ALU.not_equal, fill=1.0,
                            base=0, pattern=[[-1, HEADS]], channel_multiplier=1)
            g.affine_select(out=head_rows[:, RS:WIDE], in_=head_rows[:, RS:WIDE], compare_op=ALU.not_equal, fill=1.0,
                            base=-HEADS, pattern=[[0, N_REL]], channel_multiplier=1)
            g.tensor_scalar(looped[:], node_no[:], float(N_LOOPED), None, ALU.is_lt).then_inc(s_pool, 1)
            pool.wait_ge(s_pool, 2)
            g.tensor_scalar(loop_bias[:], looped[:], -1.0, BIG, ALU.add, ALU.mult).then_inc(s_const, 1)

            pool.wait_ge(s_plan, 1)
            turns = g.value_load(turns_i[0:1, 1:2], min_val=1, max_val=MAX_TURNS)

            def gathers(n):
                s = es[n]
                with pool.Fori(0, turns) as i:
                    for u in range(RING):
                        if n < 2:
                            pool.wait_ge(s.loaded[u], (i + 1) * (16 * edge_loads_per_step[n]))
                        else:
                            pool.wait_ge(s.idx, i * RING + (u + 1))
                        pool.sem_inc(s_passed, 1)
                        for t in range(TILES):
                            if n < 2:
                                g.indirect_dma_start(
                                    out=rows[:, u, t, 0:TABLE], out_offset=None, in_=tables[n][:, :],
                                    in_offset=bass.IndirectOffsetOnAxis(ap=src_i[:, u, t:t + 1], axis=0),
                                ).then_inc(s.gathered[u], 16)
                            else:
                                g.indirect_dma_start(
                                    out=rows[:, u, t, 0:D], out_offset=None, in_=yrows[:, :],
                                    in_offset=bass.IndirectOffsetOnAxis(ap=row_i[:, u, t:t + 1], axis=0),
                                ).then_inc(s.gathered[u], 16)

            for n in range(3):
                gathers(n)

        @block.scalar
        def _(act):
            a = nc.scalar
            for n in range(3):
                for b in range(HALVES):
                    act.sem_inc(ns[n].stored[b], 16)
            for y in range(2):
                act.sem_inc(ns[2].ystored[y], 16)
            act.wait_ge(s_plan, 1)
            turns = a.value_load(turns_i[0:1, 1:2], min_val=1, max_val=MAX_TURNS)

            def node_act(n):
                s = ns[n]

                def weights(g, b):
                    act.wait_ge(s.dist, g + 1)
                    a.activation(n_sm[:, b, 2:4, :, :], n_sm[:, b, 0:2, :, :], ACT.Exp).then_inc(s.wexp, 1)

                def elu(g, b):
                    act.wait_ge(s.conv, g + 1)
                    a.activation(n_neg[:, b, :, :], n_acc[:, b, :, 0:D], ACT.Relu, scale=-1.0).then_inc(s.neg, 1)
                    act.wait_ge(s.neg, g + 1)
                    a.activation(n_h[:, b, :, :], n_neg[:, b, :, :], ACT.Exp, scale=-1.0).then_inc(s.negexp, 1)

                def deviation(g, b):
                    act.wait_ge(s.var, g + 1)
                    a.activation(n_st[:, b, :, 8:9], n_st[:, b, :, 7:8], ACT.Sqrt, bias=eps_t[:, 0:1]).then_inc(s.std, 1)

                def transposed(g, turn, b, k):
                    j = g * GROUP + k
                    y = (b * GROUP + k) % 2
                    if n == 2:
                        act.wait_ge(s.ystored[y], (turn * GROUP + (b * GROUP + k) // 2) * 32 + 16)
                    act.wait_ge(s.hT, j + 1)
                    src_ = bank[y][:, 0:D].rearrange("p (c q) -> p c q", c=2)
                    if n == 1:
                        a.activation(n_hT[:, y, :, :], src_, ACT.Identity, bias=minus_one[:, 0:1]).then_inc(s.hTs, 1)
                    else:
                        a.activation(n_hT[:, y, :, :], src_, ACT.Relu).then_inc(s.hTs, 1)
                    if n == 2:
                        act.wait_ge(s.hTs, j + 3)
                        act.dma_start(hTd[:, :, bass.ds(j * P, P)], n_hT[:, y, :, :]).then_inc(s.ystored[y], 16)

                if n == 0:
                    deviation(0, 0)
                else:
                    weights(0, 0)
                    elu(0, 0)
                    if n == 2:
                        deviation(0, 0)
                transposed(0, 0, 0, 0)

                def group(g, turn, b, more, loops):
                    nb = 1 - b
                    if n < 2:
                        transposed(g, turn, b, 1)
                        if more:
                            if n == 0:
                                deviation(g + 1, nb)
                            elif loops:
                                weights(g + 1, nb)
                        transposed(g, turn, b, 2)
                        if more and n > 0 and not loops:
                            elu(g + 1, nb)
                        act.wait_ge(s.mm, (g + 1) * GROUP)
                        act.wait_ge(s.stored[b], turn * (16 * n_stores[n]) + 16)
                        p0 = 2 + b * GROUP
                        a.activation(n_out[:, b, :, :], psum[:, p0:p0 + GROUP, 0:TABLE], ACT.Copy).then_inc(s.prod, 1)
                        if more and n > 0 and loops:
                            elu(g + 1, nb)
                        if more:
                            transposed(g + 1, turn + b, nb, 0)
                        return
                    for k in range(GROUP):
                        j = g * GROUP + k
                        y = (b * GROUP + k) % 2
                        for q in range(4):
                            act.wait_ge(s.mm, j * 4 + (q + 1))
                            a.activation(n_y[:, y, q * 512:(q + 1) * 512], bank[2 + q][:, :], ACT.Copy).then_inc(s.copied, 1)
                            if more and loops and (k, q) == (0, 0):
                                weights(g + 1, nb)
                            if more and (k, q) == (1, 0):
                                elu(g + 1, nb)
                            if more and (k, q) == (1, 3):
                                deviation(g + 1, nb)
                            if q == 2 and k + 1 < GROUP:
                                transposed(g, turn, b, k + 1)
                            elif q == 2 and more:
                                transposed(g + 1, turn + b, nb, 0)
                        act.wait_ge(s.copied, (j + 2) * 4)
                        act.dma_start(tile_rows(yrel, j), n_y[:, y, :]).then_inc(s.ystored[y], 16)

                over_groups(act, group, n)

            def edge_act(n):
                s = es[n]
                w = width[n]

                def hot_bf16(step, u):
                    act.wait_ge(s.hot, step + 1)
                    a.activation(onehot_b[:], onehot[:, u, :, :], ACT.Copy).then_inc(s.hotb, 1)

                def hot_transposed(step):
                    act.wait_ge(s.hotT, step + 1)
                    for half, (t0, t1) in enumerate(((0, 7), (7, TILES))):
                        last = a.activation(
                            onehot_T[:, t0:t1, :],
                            bank[half].bitcast(BF16)[:, 0:(t1 - t0) * P].rearrange("p (t m) -> p t m", m=P), ACT.Copy)
                    last.then_inc(s.hotTs, 1)

                def store_out(step, slot):
                    b0 = a.value_load(prev_i[0:1, bass.ds(step, 1)], min_val=0, max_val=N_NODES)
                    act.wait_ge(s.stored, step * 16 + 16)
                    act.wait_ge(s.outw, step + (RING + 1))
                    act.dma_start(out[bass.ds(b0, P), :], out_sb[:, slot, :]).then_inc(s.stored, 16)

                def store_sums(step, u):
                    act.wait_ge(s.done, step + (RING + 1))
                    a.activation(acc_sb[:, u % 2, 0:w], bank[6 + u % 2][:, 0:w], ACT.Copy).then_inc(s.acc, 1)
                    if n < 2:
                        b0 = a.value_load(step_i[0:1, 1, bass.ds(step, 1)], min_val=0, max_val=N_NODES)
                        a.activation(fac_row[:, 0:w], bank[3][0:1, 0:w], ACT.Copy).then_inc(s.facr, 1)
                        act.wait_ge(s.stored, step * 16 + 16)
                        act.wait_ge(s.acc, step + 2)
                        act.dma_start(accs[n][bass.ds(b0, P), 0:w], acc_sb[:, u % 2, 0:w]).then_inc(s.stored, 16)

                def lay_out(step):
                    act.wait_ge(s.endsT, step + 1)
                    a.activation(seq_v[:, 0::2], bank[3][0:HEADS, 0:P], ACT.Copy)
                    a.activation(seq_v[:, 1::2], bank[3][32:32 + HEADS, 0:P], ACT.Copy)
                    a.activation(seq_c[:, 0:2 * P:2], bank[3][64:64 + HEADS, 0:P], ACT.Copy)
                    a.activation(seq_c[:, 1:2 * P:2], bank[3][96:96 + HEADS, 0:P], ACT.Copy).then_inc(s.seq, 1)

                def exponentials(step, u):
                    act.wait_ge(s.facd, step + 1)
                    a.activation(fac[0:HEADS, :], fac_d[:, :], ACT.Exp).then_inc(s.fac, 1)
                    act.wait_ge(s.expd, step + 1)
                    a.activation(rows[:, u, :, ES:MS], zz.rearrange("p h t -> p t h"), ACT.Exp).then_inc(s.exp, 1)
                    act.wait_ge(s.exp, step + 1)
                    for h in range(HEADS):
                        r = rows[:, u, ACT_TILE, h * HID:(h + 1) * HID]
                        last = a.activation(r, r, ACT.Copy, scale=rows[:, u, ACT_TILE, ES + h:ES + h + 1])
                    last.then_inc(s.share, 1)

                hot_bf16(0, 0)
                hot_transposed(0)
                if n < 2:
                    hot_bf16(1, 1)
                    lay_out(0)
                    hot_transposed(1)
                    exponentials(0, 0)
                    act.wait_ge(s.back, 1)
                    a.activation(fac_row[:, 0:w], bank[3][0:1, 0:w], ACT.Copy).then_inc(s.facr, 1)
                    hot_bf16(2, 2)
                with act.Fori(0, turns) as i:
                    for u in range(RING):
                        step = i * RING + u
                        if n < 2:
                            lay_out(step + 1)
                            hot_transposed(step + 2)
                            exponentials(step + 1, (u + 1) % RING)
                            hot_bf16(step + 3, (u + 3) % RING)
                        else:
                            hot_bf16(step + 1, (u + 1) % RING)
                            act.wait_ge(s.coef, step + 1)
                            act.wait_ge(s.gathered[u], (i + 1) * (16 * TILES))
                            r = rows[:, u, ACT_TILE, 0:D]
                            a.activation(r, r, ACT.Copy, scale=coef[:, u % 2, ACT_TILE:ACT_TILE + 1]).then_inc(s.share, 1)
                            hot_transposed(step + 1)
                            store_out(step, 1 - u % 2)
                        store_sums(step, u)
                if n == 2:
                    store_out(turns * RING, 1)

            for n in range(3):
                node_act(n)
                act.sem_inc(es[n].stored, 16)
                edge_act(n)

        @block.tensor
        def _(pe):
            t_ = nc.tensor
            for n in range(3):
                pe.sem_inc(es[n].done, RING)
            pe.wait_ge(s_const, 1)
            pe.wait_ge(s_plan_row, 1)
            for q, row in enumerate((3, 4, 5)):
                last = t_.matmul(bank[0][:, q:q + 1], plan[0:1, row, :], ones[0:1, 0:1], start=True, stop=True)
            last.then_inc(s_plan_col, 1)
            pe.wait_ge(s_plan_row, 2)
            for q, m in enumerate((0, 2, 3)):
                last = t_.matmul(bank[1 + q][:, 0:MAX_STEPS], ones[:, :], hot[:, m, :], start=True, stop=True)
            last.then_inc(s_plan_col, 1)
            pe.wait_ge(s_plan, 1)
            turns = t_.value_load(turns_i[0:1, 1:2], min_val=1, max_val=MAX_TURNS)

            def node_pe(n):
                s = ns[n]

                def transpose(g, b, k, y):
                    pe.wait_ge(s.hTs, g * GROUP + (k + 1))
                    for c in range(2):
                        last = t_.transpose(bank[y][:, c * P:(c + 1) * P], n_h[:, b, k, c * P:(c + 1) * P], ident[:])
                    last.then_inc(s.hT, 1)

                def first_transpose(g, b):
                    pe.wait_ge(s.h, g + (HALVES + 1))
                    transpose(g, b, 0, b * GROUP % 2)

                def group(g, turn, b, more, loops):
                    if n < 2:
                        pe.wait_ge(s.prod, g + 1)
                    for k in range(GROUP):
                        y = (b * GROUP + k) % 2
                        j = g * GROUP + k
                        if k + 1 < GROUP:
                            transpose(g, b, k + 1, 1 - y)
                        pe.wait_ge(s.hTs, j + 3)
                        if n < 2:
                            for c in range(2):
                                last = t_.matmul(bank[2 + b * GROUP + k][:, 0:TABLE], n_hT[:, y, c, :], wx[n][:, c, :],
                                                 start=(c == 0), stop=(c == 1))
                            last.then_inc(s.mm, 1)
                            if more and k + 1 == GROUP:
                                first_transpose(g + 1, 1 - b)
                            continue
                        for q in range(4):
                            pe.wait_ge(s.copied, j * 4 + (q + 1))
                            if q == 3 and more and k + 1 == GROUP:
                                first_transpose(g + 1, 1 - b)
                            for c in range(2):
                                last = t_.matmul(bank[2 + q][:, :], n_hT[:, y, c, :],
                                                 wrel[:, c, 2 * q:2 * q + 2, :], start=(c == 0), stop=(c == 1))
                            last.then_inc(s.mm, 1)

                first_transpose(0, 0)
                over_groups(pe, group, 0)

            def edge_pe(n):
                s = es[n]
                w = width[n]

                def transpose_hot(step):
                    pe.wait_ge(s.hotb, step + 1)
                    for t in range(TILES):
                        b, o = (0, t) if t < 7 else (1, t - 7)
                        last = t_.transpose(bank[b].bitcast(BF16)[:, o * P:(o + 1) * P], onehot_b[:, t, :], identb[:])
                    last.then_inc(s.hotT, 1)

                def look_up(step, u):
                    pe.wait_ge(s.hotTs, step + 1)
                    pe.wait_ge(s.read, step + 1)
                    if n == 2:
                        pe.wait_ge(s.prep, step * prep_steps[2] + prep_steps[2])
                    nv = 3 * HEADS if n < 2 else 3 * N_REL
                    win = win_ad if n < 2 else win_ic
                    for t in range(TILES):
                        last = t_.matmul(bank[2][:, t * nv:(t + 1) * nv], onehot_T[:, t, :], win[:, u, :], start=True, stop=True)
                    last.then_inc(s.dstv, 1)

                def add_up(step, u, t0, t1, last=False):
                    for t in range(t0, t1):
                        product = t_.matmul(bank[6 + u % 2][:, 0:w], onehot[:, u, t, :], rows[:, u, t, 0:w], start=(t == 0),
                                            stop=last)
                    return product

                def transpose_ends(step, u):
                    pe.wait_ge(s.ends, step + 1)
                    t_.transpose(bank[3][:, 0:P], edge_ends[:, u % 2, :], ident[:]).then_inc(s.endsT, 1)

                def transpose_back(step):
                    t_.transpose(bank[5][:, 0:HEADS], seq_m[:, 0::2], ident[0:HEADS, 0:HEADS])
                    t_.transpose(bank[5][:, HEADS:2 * HEADS], seq_m[:, 1::2], ident[0:HEADS, 0:HEADS]).then_inc(s.back, 1)

                def spread_factors(step):
                    pe.wait_ge(s.fac, step + 1)
                    pe.sem_inc(s_passed, 1)
                    t_.matmul(bank[3][0:1, 0:w], fac[:, :], head_rows[:, 0:w], start=True, stop=True)

                def pick_carried(step, u):
                    pe.wait_ge(s.sel, step + 1)
                    pe.wait_ge(s.acc, step + 1)
                    t_.matmul(bank[4][0:1, 0:w], sel[:, u:u + 1], acc_sb[:, 1 - u % 2, 0:w], start=True, stop=True).then_inc(s.pick, 1)

                def add_carried(step, u):
                    pe.wait_ge(s.carry, step + 1)
                    t_.matmul(bank[6 + u % 2][:, 0:w], first_row[0:1, :], carry[0:1, 0:w], start=False, stop=False)

                transpose_hot(0)
                look_up(0, 0)
                if n < 2:
                    transpose_hot(1)
                    transpose_ends(0, 0)
                    look_up(1, 1)
                    spread_factors(0)
                    pe.wait_ge(s.seqm, 1)
                    transpose_back(0)
                parts = len(DVE_PARTS)
                with pe.Fori(0, turns) as i:
                    for u in range(RING):
                        step = i * RING + u
                        if n < 2:
                            pe.wait_ge(s.facr, step + 1)
                            transpose_ends(step + 1, (u + 1) % RING)
                            transpose_hot(step + 2)
                            pe.wait_ge(s.rhs, step * parts + 1)
                            add_up(step, u, *DVE_PARTS[0])
                            pick_carried(step, u)
                            pe.wait_ge(s.seqm, step + 2)
                            pe.sem_inc(s_passed, 1)
                            transpose_back(step + 1)
                        else:
                            pe.wait_ge(s.outw, step + RING)
                            pick_carried(step, u)
                            transpose_hot(step + 1)
                            pe.wait_ge(s.rhs, step * parts + 1)
                            add_up(step, u, *DVE_PARTS[0])
                            look_up(step + 1, (u + 1) % RING)
                            for c in range(2):
                                t_.matmul(bank[3 + 2 * (u % 2)][:, 0:D], win_hT[:, u, c, :], wrel[:, c, N_REL, :],
                                          start=(c == 0), stop=(c == 1))
                        for q in range(1, parts - 1):
                            pe.wait_ge(s.rhs, step * parts + (q + 1))
                            add_up(step, u, *DVE_PARTS[q])
                        if n < 2:
                            look_up(step + 2, (u + 2) % RING)
                        add_carried(step, u)
                        pe.wait_ge(s.share, step + 1)
                        add_up(step, u, ACT_TILE, ACT_TILE + 1)
                        pe.wait_ge(s.rhs, (step + 1) * parts)
                        t0, t1 = DVE_PARTS[-1]
                        add_up(step, u, t0, t1 - 1)
                        if n < 2:
                            spread_factors(step + 1)
                        add_up(step, u, t1 - 1, t1, last=True).then_inc(s.done, 1)

            for n in range(3):
                if n == 2:
                    pe.wait_ge(s_rload, 16 * (N_REL + 1))
                node_pe(n)
                edge_pe(n)

        @block.vector
        def _(dve):
            v = nc.vector
            for n in range(3):
                dve.sem_inc(ns[n].h, HALVES)
                if n < 2:
                    dve.sem_inc(ns[n].prod, HALVES)
                dve.sem_inc(es[n].acc, 1)
                dve.sem_inc(es[n].read, 1)
                dve.sem_inc(ns[n].hTs, 2)
            dve.sem_inc(ns[2].copied, 4)
            dve.sem_inc(es[2].outw, RING)
            dve.wait_ge(s_const, 1)
            dve.wait_ge(s_ends, 16 * 2)
            nwork = [0]

            def do(ins):
                nwork[0] += 1
                ins.then_inc(s_vplan, 1)
                dve.wait_ge(s_vplan, nwork[0])

            B, E_, NW, CUM, CUX, V = range(6)
            do(v.tensor_copy(ends[:], ends_i[:]))
            do(v.memset(ends[0:1, 0, 0:1], 0.0))
            do(v.tensor_copy(plan[0:1, B, :], ends[0:1, 0, :]))
            do(v.tensor_scalar(plan[0:1, E_, 0:P - 1], ends[0:1, 0, 1:P], -1.0, None, ALU.add))
            do(v.memset(plan[0:1, E_, P - 1:P], float(N_NODES - 1)))
            do(v.tensor_scalar(ends[0:1, 1, :], ends[0:1, 1, :], float(N_NODES - 1), None, ALU.min))
            do(v.tensor_tensor(plan[0:1, E_, :], plan[0:1, E_, :], ends[0:1, 1, :], ALU.max))
            do(v.tensor_tensor(plan_i[0:1, :], plan[0:1, E_, :], plan[0:1, B, :], ALU.subtract))
            do(v.tensor_scalar(plan_i[0:1, :], plan_i[0:1, :], 7, None, ALU.arith_shift_right))
            do(v.tensor_copy(plan[0:1, NW, :], plan_i[0:1, :]))
            do(v.tensor_scalar(plan[0:1, NW, :], plan[0:1, NW, :], 1.0, None, ALU.add))
            do(v.tensor_tensor_scan(plan[0:1, CUM, :], plan[0:1, NW, :], zeros_t[0:1, 0:P], 0.0, ALU.add, ALU.add))
            do(v.tensor_tensor(plan[0:1, CUX, :], plan[0:1, CUM, :], plan[0:1, NW, :], ALU.subtract))
            do(v.tensor_scalar(plan[0:1, V, 0:1], plan[0:1, CUM, P - 1:P], float(RING - 1), None, ALU.add))
            do(v.tensor_copy(turns_i[0:1, 0:1], plan[0:1, V, 0:1]))
            do(v.tensor_scalar(turns_i[0:1, 1:2], turns_i[0:1, 0:1], 2, None, ALU.arith_shift_right))
            v.scalar_tensor_tensor(plan[0:1, V, :], plan[0:1, CUX, :], -float(P), plan[0:1, B, :], ALU.mult, ALU.add).then_inc(s_plan_row, 1)
            dve.wait_ge(s_plan_col, 1)
            do(v.tensor_copy(cols[:], bank[0][:, 0:3]))
            do(v.tensor_scalar(hot[:, 0, :], iota_steps[:], cols[:, 0:1], None, ALU.is_ge))
            do(v.tensor_scalar(hot[:, 1, :], iota_steps[:], cols[:, 1:2], None, ALU.is_ge))
            do(v.tensor_tensor(hot[:, 2, :], hot[:, 1, :], hot[:, 0, :], ALU.subtract))
            v.tensor_scalar(hot[:, 3, :], hot[:, 2, :], cols[:, 2:3], None, ALU.mult).then_inc(s_plan_row, 1)
            dve.wait_ge(s_plan_col, 2)
            do(v.tensor_scalar(hot[:, 0, :], iota_steps[:], float(P), -float(N_NODES), ALU.mult, ALU.add))
            do(v.tensor_tensor(hot[:, 0, :], hot[:, 0, :], bank[2][:, 0:MAX_STEPS], ALU.mult))
            do(v.tensor_tensor(hot[:, 0, :], hot[:, 0, :], bank[3][:, 0:MAX_STEPS], ALU.add))
            do(v.tensor_scalar(base_of[:, 1:MAX_STEPS + 1], hot[:, 0, :], float(N_NODES), None, ALU.add))
            do(v.tensor_copy(prev_i[0:1, 1:MAX_STEPS], base_of[0:1, 1:MAX_STEPS]))
            do(v.memset(prev_i[0:1, 0:1], N_NODES))
            do(v.tensor_scalar(step_i[0:1, 0, :], bank[1][0:1, 0:MAX_STEPS], float(P), None, ALU.mult))
            dve.wait_ge(s_wload, 16 * 9)
            for n in range(2):
                for q in range(2):
                    a_ = att[:, 2 * n + q, :].unsqueeze(1).to_broadcast([P, 2, D])
                    do(v.tensor_tensor(att_tmp[:], wx[n][:, :, 0:D], a_, ALU.mult))
                    do(v.tensor_reduce(wx[n][:, :, D + q * HEADS:D + (q + 1) * HEADS],
                                       att_tmp.rearrange("p k (h d) -> p k h d", h=HEADS), AX.X, ALU.add))
            v.tensor_copy(step_i[0:1, 1, :], base_of[0:1, 1:MAX_STEPS + 1]).then_inc(s_plan, 1)
            dve.wait_ge(s_plan, 1)
            turns = v.value_load(turns_i[0:1, 1:2], min_val=1, max_val=MAX_TURNS)

            def split(t, parts, value, rest, signal=None):
                t.add(v.tensor_copy(parts[:, :, :, 0], value))
                t.settle()
                t.add(v.tensor_tensor(rest, value, parts[:, :, :, 0], ALU.subtract))
                t.settle()
                t.add(v.tensor_copy(parts[:, :, :, 1], rest))
                t.settle()
                t.add(v.tensor_tensor(rest, rest, parts[:, :, :, 1], ALU.subtract))
                t.settle()
                if signal is None:
                    t.add(v.tensor_copy(parts[:, :, :, 2], rest))
                else:
                    v.tensor_copy(parts[:, :, :, 2], rest).then_inc(signal, 1)

            def heads(ap):
                return ap.rearrange("p k (h d) -> p k h d", h=HEADS)

            def node_vec(n):
                s = ns[n]
                n_loads = (1, 2, 3)[n]
                looped_turns = LOOPED_TURNS if n > 0 else 0
                per_head = (4, 17, 23)[n]
                per = (16, 42, 46)[n]
                per_plain = (16, 14, 18)[n]

                def scores(t, g, b):
                    sm, own, acc = n_sm[:, b], n_own[:, b], n_acc[:, b]
                    D_EDGE, D_LOOP, E, M, TOP = sm[:, 0], sm[:, 1], sm[:, 4], sm[:, 5], sm[:, 6]
                    dve.wait_ge(s.loaded[b], (g_turn(g) + 1) * (16 * n_loads))
                    t.add(v.tensor_tensor(E, own[:, :, D:D + HEADS], own[:, :, D + HEADS:TABLE], ALU.add))
                    t.add(v.tensor_scalar(M, acc[:, :, ES:MS], 0.0, -BIG, ALU.is_le, ALU.mult))
                    t.settle()
                    t.add(v.scalar_tensor_tensor(E, E, SLOPE, E, ALU.mult, ALU.max))
                    t.add(v.tensor_tensor(M, M, acc[:, :, MS:RS], ALU.add))
                    t.settle()
                    t.add(v.tensor_tensor(E, E, loop_bias[:, bass.ds(g[0] * GROUP, GROUP)].unsqueeze(2).to_broadcast([P, GROUP, HEADS]), ALU.add))
                    t.settle()
                    t.add(v.tensor_tensor(TOP, M, E, ALU.max))
                    t.settle()
                    t.add(v.tensor_tensor(D_EDGE, M, TOP, ALU.subtract))
                    v.tensor_tensor(D_LOOP, E, TOP, ALU.subtract).then_inc(s.dist, 1)

                def combine(t, g, b):
                    sm, own, acc = n_sm[:, b], n_own[:, b], n_acc[:, b]
                    W_EDGE, W_LOOP, DEN = sm[:, 2], sm[:, 3], sm[:, 7]
                    dve.wait_ge(s.wexp, g[0] + 1)
                    t.add(v.tensor_tensor(W_LOOP, W_LOOP, looped[:, bass.ds(g[0] * GROUP, GROUP)].unsqueeze(2).to_broadcast([P, GROUP, HEADS]), ALU.mult))
                    t.add(v.tensor_tensor(DEN, acc[:, :, ES:MS], W_EDGE, ALU.mult))
                    t.settle()
                    t.add(v.tensor_tensor(DEN, DEN, W_LOOP, ALU.add))
                    t.settle()
                    t.add(v.tensor_scalar(DEN, DEN, TINY, None, ALU.max))
                    t.settle()
                    t.add(v.reciprocal(DEN, DEN))
                    t.settle()
                    t.add(v.tensor_tensor(W_EDGE, W_EDGE, DEN, ALU.mult))
                    t.add(v.tensor_tensor(W_LOOP, W_LOOP, DEN, ALU.mult))
                    t.settle()
                    wide = [P, GROUP, HEADS, HID]
                    t.add(v.tensor_tensor(heads(acc[:, :, 0:D]), heads(acc[:, :, 0:D]), W_EDGE.unsqueeze(3).to_broadcast(wide), ALU.mult))
                    t.add(v.tensor_tensor(heads(own[:, :, 0:D]), heads(own[:, :, 0:D]), W_LOOP.unsqueeze(3).to_broadcast(wide), ALU.mult))
                    t.settle()
                    t.add(v.tensor_tensor(acc[:, :, 0:D], acc[:, :, 0:D], own[:, :, 0:D], ALU.add))
                    t.settle()
                    v.tensor_tensor(acc[:, :, 0:D], acc[:, :, 0:D], biases[:, n - 1, :].unsqueeze(1).to_broadcast([P, GROUP, D]),
                                    ALU.add).then_inc(s.conv, 1)

                def divide(t, g, b):
                    acc, DEN = n_acc[:, b], n_sm[:, b, 7]
                    dve.wait_ge(s.loaded[b], (g_turn(g) + 1) * (16 * (n_loads - 1)) + 16 * (looped_turns + 1))
                    t.add(v.tensor_scalar(DEN, acc[:, :, ES:MS], TINY, None, ALU.max))
                    t.settle()
                    t.add(v.reciprocal(DEN, DEN))
                    t.settle()
                    t.add(v.tensor_tensor(heads(acc[:, :, 0:D]), heads(acc[:, :, 0:D]),
                                          DEN.unsqueeze(3).to_broadcast([P, GROUP, HEADS, HID]), ALU.mult))
                    t.settle()
                    v.tensor_tensor(acc[:, :, 0:D], acc[:, :, 0:D], biases[:, n - 1, :].unsqueeze(1).to_broadcast([P, GROUP, D]),
                                    ALU.add).then_inc(s.conv, 1)

                def elu(t, g, b):
                    acc, h, xin, st = n_acc[:, b], n_h[:, b], n_x[:, b], n_st[:, b]
                    dve.wait_ge(s.negexp, g[0] + 1)
                    if n == 1:
                        v.scalar_tensor_tensor(h, acc[:, :, 0:D], 0.0, h, ALU.max, ALU.add).then_inc(s.h, 1)
                    else:
                        t.add(v.scalar_tensor_tensor(acc[:, :, 0:D], acc[:, :, 0:D], 0.0, h, ALU.max, ALU.add))
                        t.settle()
                        t.add(v.scalar_tensor_tensor(xin, acc[:, :, 0:D], -1.0, xin, ALU.add, ALU.add))
                        t.settle()

                def variance(t, g, b):
                    xin, st = n_x[:, b], n_st[:, b]
                    if n == 0:
                        dve.wait_ge(s.loaded[b], (g_turn(g) + 1) * (16 * n_loads))
                    for k in range(GROUP):
                        t.add(v.bn_stats(st[:, k, 0:6], xin[:, k, :]))
                    t.settle()
                    dve.sem_inc(s_passed, 1)
                    for k in range(GROUP):
                        last = v.bn_aggr(st[:, k, 6:8], st[:, k, 0:6])
                    last.then_inc(s.var, 1)

                def normalise(t, g, b):
                    xin, st, h = n_x[:, b], n_st[:, b], n_h[:, b]
                    dve.wait_ge(s.std, g[0] + 1)
                    t.add(v.reciprocal(st[:, :, 9:10], st[:, :, 8:9]))
                    t.settle()
                    for k in range(GROUP):
                        last = v.tensor_scalar(h[:, k, :], xin[:, k, :], st[:, k, 6:7], st[:, k, 9:10], ALU.subtract, ALU.mult)
                    last.then_inc(s.h, 1)

                def residual(t, g, b):
                    dve.wait_ge(s.stored[b], g_turn(g) * (16 * n_stores[n]) + 16)
                    v.tensor_tensor(n_out[:, b, :, 0:D], n_x[:, b], biases[:, 2, :].unsqueeze(1).to_broadcast([P, GROUP, D]),
                                    ALU.add).then_inc(s.res, 1)
                    dve.wait_ge(s.res, g[0] + 1)

                def results(t, g, b):
                    dve.wait_ge(s.prod, g[0] + (HALVES + 1))
                    split(t, n_adp[:, b].rearrange("p k (h q) -> p k h q", q=3), n_out[:, b, :, D + HEADS:TABLE], n_sm[:, b, 8], s.res)

                def g_turn(g):
                    return g[1]

                def convolved(t, g, b, loops):
                    if loops:
                        scores(t, g, b)
                        combine(t, g, b)
                    else:
                        divide(t, g, b)

                def node_head():
                    t = Turn(dve, s.vec, per_head, 0)
                    g = (0, 0)
                    if n > 0:
                        convolved(t, g, 0, True)
                        elu(t, g, 0)
                    if n != 1:
                        variance(t, g, 0)
                        if n == 2:
                            residual(t, g, 0)
                        normalise(t, g, 0)
                    t.end()

                def group(t, g, b, more, loops):
                    nb = 1 - b
                    nxt = (g[0] + 1, g[1] + b)
                    if n == 0:
                        if more:
                            variance(t, nxt, nb)
                            normalise(t, nxt, nb)
                        results(t, g, b)
                    elif n == 1:
                        if more:
                            convolved(t, nxt, nb, loops)
                        if more and not loops:
                            elu(t, nxt, nb)
                        results(t, g, b)
                        if more and loops:
                            elu(t, nxt, nb)
                    else:
                        if more:
                            convolved(t, nxt, nb, loops)
                        if more:
                            elu(t, nxt, nb)
                            variance(t, nxt, nb)
                            residual(t, nxt, nb)
                            normalise(t, nxt, nb)

                node_head()
                if looped_turns:
                    with dve.Fori(0, looped_turns) as i:
                        t = Turn(dve, s.vec, per, i, per_head)
                        for b in range(HALVES):
                            group(t, (i * HALVES + b, i), b, True, True)
                        t.end()
                before = per_head + looped_turns * (per - per_plain)
                with dve.Fori(looped_turns, NODE_TURNS) as i:
                    t = Turn(dve, s.vec, per_plain, i, before)
                    for b in range(HALVES):
                        group(t, (i * HALVES + b, i), b, True, False)
                    t.end()
                t = Turn(dve, s.vec, per_plain, NODE_TURNS, before)
                for g in range(NODE_TURNS * HALVES, NODE_GROUPS):
                    group(t, (g, NODE_TURNS), g % HALVES, g + 1 < NODE_GROUPS, False)

            HT = [P, HEADS, TILES]

            def over_heads(ap):
                return ap.unsqueeze(1).to_broadcast(HT)

            def over_tiles(ap):
                return ap.unsqueeze(2).to_broadcast(HT)

            def edge_vec(n):
                s = es[n]
                w = width[n]
                per_prep = prep_steps[n]
                per_vec = (11, 11, 3)[n]
                L = HEADS * (TILES + 1)

                def prepare(step, u, turn):
                    t = Turn(dve, s.prep, per_prep, step)
                    kf = keyf[:, u, :]
                    base = base_of[:, bass.ds(step + 1, 1)]
                    dve.wait_ge(s.loaded[u], (turn + 1) * (16 * edge_loads_per_step[n]))
                    t.add(v.tensor_scalar(kf, key_i[:, u, :], base, None, ALU.subtract))
                    t.settle()
                    v.tensor_tensor(onehot[:, u, :, :], kf[:, 1:TILES + 1].unsqueeze(2).to_broadcast([P, TILES, P]),
                                    iota_win[:].unsqueeze(1).to_broadcast([P, TILES, P]), ALU.is_equal).then_inc(s.hot, 1)
                    v.tensor_scalar(sel[:, u:u + 1], iota_part[:], base_of[:, bass.ds(step, 1)], base,
                                    ALU.add, ALU.is_equal).then_inc(s.sel, 1)
                    if n < 2:
                        df = differ[:, u % 2, :]
                        t.add(v.tensor_tensor(df, kf[:, 1:KEYS], kf[:, 0:KEYS - 1], ALU.not_equal))
                        t.add(v.tensor_scalar(edge_ends[:, u % 2, 96:96 + HEADS], kf[:, TILES:TILES + 1].to_broadcast([P, HEADS]),
                                              kf[:, 1:2], -BIG, ALU.not_equal, ALU.mult))
                        t.add(v.tensor_scalar(not_first[:, u % 2, :], kf[:, 1:TILES + 1], kf[:, 1:2], -BIG, ALU.not_equal, ALU.mult))
                        t.add(v.tensor_scalar(not_final[:, u % 2, :], kf[:, 1:TILES + 1], kf[:, TILES:TILES + 1], -BIG, ALU.not_equal, ALU.mult))
                        if n == 0:
                            t.add(v.tensor_tensor(rows[:, u, :, RS:WIDE], typ_i[:, u, :].unsqueeze(2).to_broadcast([P, TILES, N_REL]),
                                                  iota_rel[:].unsqueeze(1).to_broadcast([P, TILES, N_REL]), ALU.is_equal))
                        t.settle()
                        t.add(v.tensor_scalar(by_head(cut[:, u % 2, 0:L])[:, :, 1:TILES],
                                              df[:, 1:TILES].unsqueeze(1).to_broadcast([P, HEADS, TILES - 1]), -BIG, None, ALU.mult))
                        t.add(v.tensor_scalar(edge_ends[:, u % 2, 64:64 + HEADS], df[:, 0:1].to_broadcast([P, HEADS]), -BIG, None, ALU.mult))
                    else:
                        cnt, rest = cnt_rest[:, 0:1, :], cnt_rest[:, 1:2, :]
                        t.add(v.tensor_scalar(cnt, win_cnt[:, u:u + 1, :], 1.0, None, ALU.max))
                        t.settle()
                        t.add(v.reciprocal(cnt, cnt))
                        t.settle()
                        split(t, win_ic[:, u, :].rearrange("p (k r q) -> p k r q", k=1, q=3), cnt, rest)
                    t.end()

                def row_numbers(u, turn):
                    dve.wait_ge(s.loaded[u], (turn + 1) * (16 * edge_loads_per_step[n]))
                    v.scalar_tensor_tensor(row_i[:, u, :], src_i[:, u, :], float(N_REL), typ_i[:, u, :],
                                           ALU.mult, ALU.add).then_inc(s.idx, 1)

                def out_window(step, u):
                    dve.wait_ge(s.acc, step + 2)
                    o = out_sb[:, u % 2, :]
                    v.tensor_tensor(o, bank[6 + u % 2][:, 0:D], win_res[:, u, :], ALU.add).then_inc(s.outp, 1)
                    dve.wait_ge(s.outp, step + 2)
                    v.tensor_tensor(o, o, bank[3 + 2 * (u % 2)][:, 0:D], ALU.add).then_inc(s.outw, 1)

                def go(ins):
                    t.add(ins)
                    t.settle()

                scv = by_head(sc[:, :])[:, :, 0:TILES]
                rm = by_head(run_m[:, :])[:, :, 0:TILES]

                def run_maxima(step, u, gathers):
                    cu = cut[:, u % 2, :]
                    dve.wait_ge(s.dstv, step + 1)
                    v.tensor_reduce(z[:], bank[2][:, 0:TILES * 3 * HEADS].rearrange("p (t h q) -> p t h q", h=HEADS, q=3),
                                    AX.X, ALU.add).then_inc(s.read, 1)
                    dve.wait_ge(s.read, step + 2)
                    dve.wait_ge(s.gathered[u], gathers * (16 * TILES))
                    go(v.tensor_tensor(zz.rearrange("p h t -> p t h"), z[:], rows[:, u, :, D:D + HEADS], ALU.add))
                    go(v.scalar_tensor_tensor(scv, zz[:], SLOPE, zz[:], ALU.mult, ALU.max))
                    go(v.tensor_tensor_scan(run_f[:], cu[:, 0:L], sc[:], -BIG, ALU.add, ALU.max))
                    go(v.tensor_tensor_scan(run_m[:, ::-1], cu[:, L:0:-1], run_f[:, ::-1], -BIG, ALU.add, ALU.max))
                    t.add(v.tensor_copy(edge_ends[:, u % 2, 0:HEADS], rm[:, :, 0]))
                    v.tensor_copy(edge_ends[:, u % 2, 32:32 + HEADS], rm[:, :, TILES - 1]).then_inc(s.ends, 1)

                def sequence_maxima(step, u):
                    dve.wait_ge(s.seq, step + 1)
                    before = seq_f[:, 1 - u % 2, 2 * P - 1:2 * P]
                    go(v.tensor_tensor_scan(seq_f[:, u % 2, :], seq_c[:, 0:2 * P], seq_v[:], before, ALU.add, ALU.max))
                    v.tensor_tensor_scan(seq_m[:, ::-1], seq_c[:, 2 * P:0:-1], seq_f[:, u % 2, ::-1], -BIG, ALU.add, ALU.max).then_inc(s.seqm, 1)
                    dve.wait_ge(s.seqm, step + 1)
                    v.tensor_scalar(fac_d[:], before, seq_m[:, 0:1], 0.0, ALU.subtract, ALU.min).then_inc(s.facd, 1)

                def exponents(step, u):
                    dve.wait_ge(s.back, step + 1)
                    tm = by_head(tmp_m[:, :])[:, :, 0:TILES]
                    tn = tmp_n[:]
                    t.add(v.tensor_tensor(tm, over_tiles(bank[5][:, 0:HEADS]), over_heads(not_first[:, u % 2, :]), ALU.add))
                    go(v.tensor_tensor(tn, over_tiles(bank[5][:, HEADS:2 * HEADS]), over_heads(not_final[:, u % 2, :]), ALU.add))
                    go(v.tensor_tensor(tm, tm, tn, ALU.max))
                    go(v.tensor_tensor(rm, rm, tm, ALU.max))
                    v.tensor_tensor(zz[:], scv, rm, ALU.subtract).then_inc(s.expd, 1)
                    t.add(v.tensor_tensor(rows[:, u, :, MS:RS], by_head(run_m[:, :]).rearrange("p h t -> p t h")[:, 0:TILES, :],
                                          differ[:, u % 2, 1:TILES + 1].unsqueeze(2).to_broadcast([P, TILES, HEADS]), ALU.mult))
                    t.settle()

                if n == 2:
                    row_numbers(0, 0)
                    row_numbers(1, 0)
                    do(v.memset(bank[7][:, 0:D], 0.0))
                    do(v.memset(bank[5][:, 0:D], 0.0))
                    prepare(0, 0, 0)
                else:
                    prepare(0, 0, 0)
                    prepare(1, 1, 0)
                    t = Turn(dve, s.vec, per_vec, 0)
                    run_maxima(0, 0, 1)
                    sequence_maxima(0, 0)
                    exponents(0, 0)
                    t.end()
                    prepare(2, 2, 0)
                with dve.Fori(0, turns) as i:
                    for u in range(RING):
                        step = i * RING + u
                        turn = i if u + 1 < RING else i + 1
                        if n < 2:
                            nxt, nu = step + 1, (u + 1) % RING
                            t = Turn(dve, s.vec, per_vec, nxt)
                            dve.wait_ge(s.exp, step + 1)
                            run_maxima(nxt, nu, i + 1 if u + 1 < RING else (i + 1) % turns + 1)
                            for t0, t1 in DVE_PARTS:
                                r = rows[:, u, t0:t1, 0:D].rearrange("p t (h d) -> p t h d", h=HEADS)
                                v.tensor_tensor(r, r, rows[:, u, t0:t1, ES:MS].unsqueeze(3).to_broadcast([P, t1 - t0, HEADS, HID]),
                                                ALU.mult).then_inc(s.rhs, 1)
                            sequence_maxima(nxt, nu)
                            dve.wait_ge(s.facr, step + 1)
                            dve.wait_ge(s.pick, step + 1)
                            v.tensor_tensor(carry[:, 0:w], fac_row[:, 0:w], bank[4][0:1, 0:w], ALU.mult).then_inc(s.carry, 1)
                            exponents(nxt, nu)
                            prepare(step + 3, (u + 3) % RING, i if u + 3 < RING else i + 1)
                        else:
                            t = Turn(dve, s.vec, per_vec, step)
                            co = coef[:, u % 2, :]
                            row_numbers((u + 2) % RING, i if u + 2 < RING else i + 1)
                            go(v.tensor_tensor(typ_hot[:], typ_i[:, u, :].unsqueeze(2).to_broadcast([P, TILES, N_REL]),
                                               iota_rel[:].unsqueeze(1).to_broadcast([P, TILES, N_REL]), ALU.is_equal))
                            dve.wait_ge(s.dstv, step + 1)
                            v.tensor_reduce(ic[:], bank[2][:, 0:TILES * 3 * N_REL].rearrange("p (t r q) -> p t r q", r=N_REL, q=3),
                                            AX.X, ALU.add).then_inc(s.read, 1)
                            dve.wait_ge(s.read, step + 2)
                            go(v.tensor_tensor(ic[:], ic[:], typ_hot[:], ALU.mult))
                            go(v.tensor_reduce(co, ic[:], AX.X, ALU.add))
                            v.tensor_tensor(co, co, wts[:, u, :], ALU.mult).then_inc(s.coef, 1)
                            prepare(step + 1, (u + 1) % RING, turn)
                            dve.wait_ge(s.coef, step + 1)
                            dve.wait_ge(s.gathered[u], (i + 1) * (16 * TILES))
                            for q, (t0, t1) in enumerate(DVE_PARTS):
                                r = rows[:, u, t0:t1, 0:D]
                                v.tensor_tensor(r, r, co[:, t0:t1].unsqueeze(2).to_broadcast([P, t1 - t0, D]), ALU.mult).then_inc(s.rhs, 1)
                                if q == 0:
                                    dve.wait_ge(s.pick, step + 1)
                                    v.tensor_copy(carry[0:1, 0:D], bank[4][0:1, 0:D]).then_inc(s.carry, 1)
                                    out_window(step - 1, (u - 1) % RING)
                        t.end()
                if n == 2:
                    out_window(turns * RING - 1, RING - 1)
                else:
                    dve.wait_ge(s.prep, turns * (RING * per_prep) + 3 * per_prep)
                    dve.sem_inc(s_prepared, 1)

            for n in range(3):
                node_vec(n)
                edge_vec(n)


def kernel(**inputs):
    import numpy as _np
    import concourse.bacc as _bacc
    from concourse import mybir as _mybir
    from concourse.bass_utils import run_bass_kernel_spmd as _run

    a = {k: _np.ascontiguousarray(v) for k, v in inputs.items()}
    pad = (N_CHUNKS + 1) * CHUNK - N_EDGES

    def padded(v, value):
        return _np.concatenate([v, _np.full(pad, value, v.dtype)])

    def in_partitions(v):
        return v.reshape(-1, TILES)

    keys = padded(a["dst"], PAD_KEY)
    before = _np.concatenate([_np.full(1, -1, keys.dtype), keys])[:-1]
    after = _np.concatenate([keys, _np.full(1, PAD_KEY, keys.dtype)])[1:]
    host = {
        "x": _np.concatenate([a["x"], _np.zeros((NP - N_NODES, D), a["x"].dtype)]),
        "edge_records": _np.concatenate([
            in_partitions(before)[:, :1], in_partitions(keys), in_partitions(after)[:, -1:],
            in_partitions(padded(a["src"], 0)), in_partitions(padded(a["edge_type_8"], 0))], axis=1),
        "chunk_firsts": keys[None, 0:N_CHUNKS * CHUNK:CHUNK],
        "chunk_lasts": keys[None, CHUNK - 1:N_CHUNKS * CHUNK:CHUNK],
        "edge_weight": in_partitions(padded(a["edge_weight"], 0)),
    }
    for k in ("W1", "att_src1", "att_dst1", "b1", "W2", "att_src2", "att_dst2", "b2"):
        host[k] = a["L0_gnn_" + k]
    for k in ("weight", "root", "bias"):
        host[k] = a["L1_gnn_" + k]

    nc = _bacc.Bacc("TRN2", target_bir_lowering=False, num_devices=1)
    arrays, args = {}, []
    for name, v in host.items():
        arrays[f"in_{name}"] = v = _np.ascontiguousarray(v)
        args.append(nc.dram_tensor(f"in_{name}", v.shape, _mybir.dt.from_np(v.dtype), kind="ExternalInput").ap())
    args.append(nc.dram_tensor("out_0", (NP, D), _mybir.dt.float32, kind="ExternalOutput").ap())
    build(nc, *args)
    r = _run(nc, [arrays], core_ids=[0])
    return r.results[0]["out_0"][:N_NODES]
```
